# Optimizing a Trainium2 kernel written in Bass

```python
import numpy as np
import jax
import jax.numpy as jnp

def _softmax(x, axis=-1):
    return jax.nn.softmax(x, axis=axis)

def _gelu(x):
    return jax.nn.gelu(x, approximate=True)

def _silu(x):
    return jax.nn.silu(x)

def _sigmoid(x):
    return jax.nn.sigmoid(x)

def _layernorm(x, axis=-1, eps=1e-05):
    m = jnp.mean(x, axis=axis, keepdims=True)
    v = jnp.var(x, axis=axis, keepdims=True)
    return (x - m) / jnp.sqrt(v + eps)

def _scatter_add(tgt, idx, src, axis=0):
    return tgt.at[idx].add(src)

def _segment_sum(src, seg, n):
    return jax.ops.segment_sum(src, seg, n)
kernel_name = 'mk_prb_d1_jaxref_r8_713634'

def setup_inputs(seed: int=0):
    np.random.seed(seed)
    _w = jnp.asarray

    def _L0_attn_setup():
        import math
        import jax, jax.numpy as jnp
        import numpy as np
        D_MODEL = 128
        N_HEADS = 16
        HEAD_DIM = D_MODEL // N_HEADS

        def build_rope_cache(seq_len, head_dim):
            half = head_dim // 2
            inv_freq = 1.0 / 10000.0 ** (jnp.arange(half, dtype=jnp.float32) / half)
            pos = jnp.arange(seq_len, dtype=jnp.float32)
            angles = jnp.outer(pos, inv_freq)
            return (jnp.cos(angles)[None, None], jnp.sin(angles)[None, None])

        def apply_rope(x, cos, sin):
            half = x.shape[-1] // 2
            x1, x2 = (x[..., :half], x[..., half:])
            return jnp.concatenate((x1 * cos - x2 * sin, x1 * sin + x2 * cos), axis=-1)
        key = jax.random.key(seed)
        ks = jax.random.split(key, 5)
        B, S = (2, 256)
        bound = 1.0 / math.sqrt(D_MODEL)
        x = jax.random.normal(ks[0], (B, S, D_MODEL), dtype=jnp.float32)
        qkv_w = jax.random.uniform(ks[1], (3 * D_MODEL, D_MODEL), minval=-bound, maxval=bound, dtype=jnp.float32)
        qkv_b = jax.random.uniform(ks[2], (3 * D_MODEL,), minval=-bound, maxval=bound, dtype=jnp.float32)
        out_w = jax.random.uniform(ks[3], (D_MODEL, D_MODEL), minval=-bound, maxval=bound, dtype=jnp.float32)
        out_b = jax.random.uniform(ks[4], (D_MODEL,), minval=-bound, maxval=bound, dtype=jnp.float32)
        return {'x': x, 'qkv_w': qkv_w, 'qkv_b': qkv_b, 'out_w': out_w, 'out_b': out_b}
    _L0_attn_in = _L0_attn_setup()

    def _L0_ffn_setup():
        import jax, jax.numpy as jnp
        import numpy as np
        TOP_K = 2
        key = jax.random.key(seed)
        ks = jax.random.split(key, 6)
        B, S, D, F, E = (2, 256, 128, 512, 8)
        sd = 1.0 / np.sqrt(D)
        sf = 1.0 / np.sqrt(F)
        return {'x': jax.random.normal(ks[0], (B, S, D), jnp.float32), 'gate_w': jax.random.normal(ks[1], (D, E), jnp.float32) * sd, 'w1': jax.random.normal(ks[2], (E, D, F), jnp.float32) * sd, 'b1': jax.random.normal(ks[3], (E, F), jnp.float32) * 0.01, 'w2': jax.random.normal(ks[4], (E, F, D), jnp.float32) * sf, 'b2': jax.random.normal(ks[5], (E, D), jnp.float32) * 0.01}
    _L0_ffn_in = _L0_ffn_setup()
    _d = {'L0_attn_x': _L0_attn_in['x'], 'L0_attn_qkv_w': _L0_attn_in['qkv_w'], 'L0_attn_qkv_b': _L0_attn_in['qkv_b'], 'L0_attn_out_w': _L0_attn_in['out_w'], 'L0_attn_out_b': _L0_attn_in['out_b'], 'L0_ffn_gate_w': _L0_ffn_in['gate_w'], 'L0_ffn_w1': _L0_ffn_in['w1'], 'L0_ffn_b1': _L0_ffn_in['b1'], 'L0_ffn_w2': _L0_ffn_in['w2'], 'L0_ffn_b2': _L0_ffn_in['b2']}
    _x0 = _d['L0_attn_x']
    _d['L0_attn_x'] = jax.random.normal(jax.random.fold_in(jax.random.key(seed), 1), (8, 512, 128), dtype=_x0.dtype)
    del _x0
    return _d

def reference(L0_attn_x, L0_attn_qkv_w, L0_attn_qkv_b, L0_attn_out_w, L0_attn_out_b, L0_ffn_gate_w, L0_ffn_w1, L0_ffn_b1, L0_ffn_w2, L0_ffn_b2):

    def _L0_attn_ref(x, qkv_w, qkv_b, out_w, out_b):
        import math
        import jax, jax.numpy as jnp
        import numpy as np
        D_MODEL = 128
        N_HEADS = 16
        HEAD_DIM = D_MODEL // N_HEADS

        def build_rope_cache(seq_len, head_dim):
            half = head_dim // 2
            inv_freq = 1.0 / 10000.0 ** (jnp.arange(half, dtype=jnp.float32) / half)
            pos = jnp.arange(seq_len, dtype=jnp.float32)
            angles = jnp.outer(pos, inv_freq)
            return (jnp.cos(angles)[None, None], jnp.sin(angles)[None, None])

        def apply_rope(x, cos, sin):
            half = x.shape[-1] // 2
            x1, x2 = (x[..., :half], x[..., half:])
            return jnp.concatenate((x1 * cos - x2 * sin, x1 * sin + x2 * cos), axis=-1)
        B, S, D = x.shape
        H, Hd = (N_HEADS, HEAD_DIM)
        qkv = x @ qkv_w.T + qkv_b
        qkv = qkv.reshape(B, S, 3, H, Hd).transpose(2, 0, 3, 1, 4)
        q, k, v = (qkv[0], qkv[1], qkv[2])
        cos, sin = build_rope_cache(S, Hd)
        q = apply_rope(q, cos, sin)
        k = apply_rope(k, cos, sin)
        scores = jnp.einsum('bhqd,bhkd->bhqk', q, k) / math.sqrt(Hd)
        causal = jnp.triu(jnp.ones((S, S), dtype=bool), k=1)
        scores = jnp.where(causal, jnp.finfo(scores.dtype).min, scores)
        attn = jax.nn.softmax(scores, axis=-1)
        out = jnp.einsum('bhqk,bhkd->bhqd', attn, v)
        out = out.transpose(0, 2, 1, 3).reshape(B, S, D)
        return out @ out_w.T + out_b

    def _L0_ffn_ref(x, gate_w, w1, b1, w2, b2):
        import jax, jax.numpy as jnp
        import numpy as np
        TOP_K = 2
        B, S, D = x.shape
        T = B * S
        xf = x.reshape(T, D)
        gate_scores = jax.nn.softmax(xf @ gate_w, axis=-1)
        topk_scores, topk_idx = jax.lax.top_k(gate_scores, TOP_K)
        topk_scores = topk_scores / jnp.sum(topk_scores, axis=-1, keepdims=True)
        h = jax.nn.gelu(jnp.einsum('td,edf->etf', xf, w1) + b1[:, None, :], approximate=False)
        y = jnp.einsum('etf,efd->etd', h, w2) + b2[:, None, :]
        tok = jnp.arange(T)
        y_sel = y[topk_idx.T, tok[None, :]]
        out = jnp.einsum('kt,ktd->td', topk_scores.T, y_sel)
        return out.reshape(B, S, D)
    x = L0_attn_x
    xn = _layernorm(x, axis=-1)
    x = x + _L0_attn_ref(xn, L0_attn_qkv_w, L0_attn_qkv_b, L0_attn_out_w, L0_attn_out_b) + _L0_ffn_ref(xn, L0_ffn_gate_w, L0_ffn_w1, L0_ffn_b1, L0_ffn_w2, L0_ffn_b2)
    return x

_drawn_inputs = setup_inputs


def setup_inputs(seed=0):
    import zlib

    import numpy as np

    out = dict(_drawn_inputs(seed))
    spreads = {}
    factors = {'L0_ffn_b1': 8.0, 'L0_ffn_b2': 8.0}
    for name, (base, spread) in spreads.items():
        noise = np.random.default_rng([zlib.crc32(name.encode()), seed]).standard_normal(out[name].shape)
        drawn = base * np.exp(spread * noise) if base else spread * noise
        out[name] = jnp.asarray(drawn.astype(out[name].dtype))
    for name, factor in factors.items():
        out[name] = (out[name] * factor).astype(out[name].dtype)
    return out
```

```python
import math
from contextlib import ExitStack

import numpy as np

import concourse.bass as bass
from concourse import mybir

F32 = mybir.dt.float32
F32R = mybir.dt.float32r
BF16 = mybir.dt.bfloat16
ALU = mybir.AluOpType
ACT = mybir.ActivationFunctionType
AX = mybir.AxisListType

NB, S, D = 8, 512, 128
H, HD = 16, 8
HALF = HD // 2
P = 128
TJ = S // P
NT = NB * TJ
G = 4
NI = H // G
E, F = 8, 512
EPS = 1e-5
SCALE = 1.0 / math.sqrt(HD)
NEG = -1e38
SLOTS = 2
ST_BANKS = 3
UNITS = 12
CHUNKS = [[(0, 0, 512)], [(0, 1, 384)], [(0, 2, 256), (256, 3, 128)]]
CHUNK_AT, CHUNK_W = [0, 512, 896], [512, 384, 384]
PW = sum(CHUNK_W)
BLOCKS = (2 * NB * S + E * (P - 1)) // P + 1
TURN = 4
BLOCKS += -BLOCKS % TURN
FC = F // P
PIECES = 5 * 16


def rope_tables():
    inv = (1.0 / 10000.0 ** (np.arange(HALF, dtype=np.float32) / np.float32(HALF))).astype(np.float32)
    angle = np.outer(np.arange(S, dtype=np.float32), inv).astype(np.float32)
    cos, sin = np.cos(angle).T, np.sin(angle).T
    cos8 = np.concatenate([cos, cos], 0)
    sin8 = np.concatenate([-sin, sin], 0)
    return np.tile(np.stack([cos8, sin8], 1), (H, 1, 1)).astype(np.float32)


def routing_tables():
    return np.concatenate([np.tile(np.arange(E, 0, -1), (P, 1)), np.tile(np.arange(BLOCKS), (P, 1)),
                           np.ones((P, P)), np.triu(np.ones((P, P)), 1)], 1).astype(np.float32)


class Batch:

    def __init__(self, n, turn=None):
        self.n, self.turn = n, turn

    def at(self, count, each):
        return count if self.turn is None else self.turn * int(2 * each) + count

    def plus(self, k):
        return Batch(self.n + k, self.turn)




PAIRS = 6


def slots_of(n):
    more, most = n + 1 < NB, n + 2 < NB
    extras = [("QQ", most), ("KK", most), ("AT", n > 0), ("OP", n > 0)]
    out = []
    for i in range(NI):
        pairs = [[("S", i, p)] if more else [] for p in range(PAIRS)]
        if not more and i == 0:
            pairs[1] = [("S", i, 1)]
        name, there = extras[i]
        out += pairs[0] + pairs[1] + pairs[2] + pairs[3] + ([name] if there else []) + pairs[4]
        out += ([("N", i)] if i > 0 or n > 0 else []) + pairs[5] + (["V"] if i == 3 and more else [])
    return out


PRO = [("XT", 0), ("XT", 1)] + [(k, 0) for k in ("QQ", "KK", "V")] + [(k, 1) for k in ("QQ", "KK")]
PRO += [("XT", b) for b in range(2, NB)] + ["GT"] + [("S", i, p) for i in range(NI) for p in range(PAIRS)]
EPI = ["N", "AT", "OP"]
START = [len(PRO)]
for _n in range(NB):
    START.append(START[-1] + len(slots_of(_n)))
FULL = len(slots_of(1))
assert all(len(slots_of(n)) == FULL for n in range(1, NB - 2))


def slot(key, b=None, where=None):
    if where == "pro":
        s = PRO.index(key)
    elif where == "epi":
        s = START[NB] + EPI.index(key)
    else:
        s = START[b.n] + slots_of(b.n).index(key)
        return s % SLOTS, b.at(s // SLOTS + 1, FULL / SLOTS)
    return s % SLOTS, s // SLOTS + 1


def block_kernel(nc, x, wqkv, qkb, vb, wo, ob, rope, gw, w1, w2, b2, route, out):
    keep = ExitStack()
    with keep:
        acc = keep.enter_context(nc.sbuf_tensor("acc", [P, NT, D], F32))
        xn = keep.enter_context(nc.sbuf_tensor("xn", [P, NT, D], F32))
        logits = keep.enter_context(nc.sbuf_tensor("logits", [P, NT, E], F32))
        ident = keep.enter_context(nc.sbuf_tensor("ident", [P, P], F32))
        attention(nc, x, wqkv, qkb, vb, wo, ob, rope, gw, acc, xn, logits, ident)
        experts(nc, w1, w2, b2, route, acc, xn, logits, ident, out)


def attention(nc, x, wqkv, qkb, vb, wo, ob, rope, gw, acc, xn, logits, ident):
    ctx = ExitStack()
    with ctx:
        def sb(name, shape, dt=F32):
            return ctx.enter_context(nc.sbuf_tensor(name, shape, dt))

        def sem(name):
            return ctx.enter_context(nc.semaphore(name))

        xnT = sb("xnT", [P, NB * S])
        stacks = [sb(f"stack{p}", [P, 2, NI, S], F32R) for p in range(2)]
        stack_q, stack_k = ([t[:, w] for t in stacks] for w in range(2))
        v32 = [sb(f"v32_{p}", [P, TJ, H, 32]) for p in range(2)]
        probs = [sb(f"probs{p}", [P, G, PW]) for p in range(2)]
        xTb = [sb(f"xTb{p}", [P, S]) for p in range(2)]
        ev = sb("ev", [P, 4, S])
        qk = sb("qk", [P, 2, S])
        halves = sb("halves", [P, 4, S], F32R)
        high, low = (halves[:, 2], halves[:, 1]), (halves[:, 0], halves[:, 3])
        rope_sb = sb("rope_sb", [P, 2, S])
        w_sb = sb("w_sb", [P, 5 * D])
        wo_sb = sb("wo_sb", [P, D])
        gw_sb = sb("gw_sb", [P, E])
        qkb_sb = sb("qkb_sb", [P, 4])
        vb_sb = sb("vb_sb", [P, D])
        ob_sb = sb("ob_sb", [P, D])
        o_sb = [sb(f"o_sb{p}", [P, S]) for p in range(2)]
        attn = [sb(f"attn{p}", [P, TJ, D]) for p in range(2)]
        attnT = sb("attnT", [P, S])
        stats = sb("stats", [P, NT, 6])
        mv = sb("mv", [P, NT, 2])
        rstd = sb("rstd", [P, NT])
        half = sb("half", [P, TJ])
        part = [sb(f"part{p}", [P, G, 3]) for p in range(2)]
        nm = [sb(f"nm{p}", [P, G, TJ]) for p in range(2)]
        mrow = [sb(f"mrow{p}", [G * TJ, 2, P], F32R) for p in range(NI)]
        zeros = sb("zeros", [32, S], F32R)
        rec = sb("rec", [P, TJ, G])
        identb = sb("identb", [P, P], BF16)
        maskb = sb("maskb", [P, 2, P], BF16)

        st = ctx.enter_context(nc.psum_tensor("st", [P, ST_BANKS, 512], F32))
        wk = ctx.enter_context(nc.psum_tensor("wk", [P, SLOTS, 2, 512], F32))
        po = ctx.enter_context(nc.psum_tensor("po", [P, 512], F32))

        s_x = [sem(f"s_x{b}") for b in range(NB)]
        s_c = sem("s_c")
        s_ones = sem("s_ones")
        s_consts = sem("s_consts")
        s_stat = sem("s_stat")
        s_eps = sem("s_eps")
        s_rstd = sem("s_rstd")
        s_xn = sem("s_xn")
        s_chain = sem("s_chain")
        s_pc = sem("s_pc")
        s_xr = sem("s_xr")
        s_xnT = sem("s_xnT")
        xtb = [sem(f"xtb{p}") for p in range(2)]
        wk_full = [sem(f"wk_full{k}") for k in range(SLOTS)]
        wk_free = [sem(f"wk_free{k}") for k in range(SLOTS)]
        st_full = sem("st_full")
        exp_done = sem("exp_done")
        masked = sem("masked")
        pv_done = sem("pv_done")
        o_evac = sem("o_evac")
        v_ready = sem("v_ready")
        ev_done = sem("ev_done")
        roped = sem("roped")
        split = sem("split")
        stacked = [sem(f"stacked{i}") for i in range(NI)]
        part_done = sem("part_done")
        nm_done = sem("nm_done")
        mrow_done = sem("mrow_done")
        mstored = sem("mstored")
        mrows = [sem(f"mrows{i}") for i in range(NI)]
        attn_done = sem("attn_done")
        attnT_done = sem("attnT_done")
        acc_done = sem("acc_done")
        s_out = sem("s_out")
        s_zero = sem("s_zero")
        s_red = sem("s_red")
        s_rp = sem("s_rp")
        s_nt = sem("s_nt")
        s_op = sem("s_op")
        s_mt = sem("s_mt")
        s_vz = sem("s_vz")
        s_mv = sem("s_mv")
        s_hi = sem("s_hi")
        s_mh = sem("s_mh")
        s_rec = sem("s_rec")
        s_at = sem("s_at")

        x_v = x.rearrange("b (j p) d -> p b j d", p=P)
        m_dram = nc.dram_tensor("m_dram", (NI, 2, G * TJ, P), F32, kind="Internal").ap()
        N_CONST = 7 * 16

        def wait(eng, s, v):
            if not (isinstance(v, int) and v <= 0):
                eng.wait_ge(s, v)

        def qrow(t, i, r, n=HD):
            return t.rearrange("(g r) i t -> i r g t", g=G)[i, r:r + n]


        def loops(eng, step):
            for n in range(NB):
                step(Batch(n))

        block = ctx.enter_context(nc.Block())

        @block.sync
        def _(sp):
            sp.dma_start(acc[:, 0:TJ, :], x_v[:, 0]).then_inc(s_x[0], 16)
            sp.dma_start(w_sb[:, :], wqkv).then_inc(s_c, 16)
            sp.dma_start(qkb_sb[:, :], qkb).then_inc(s_c, 16)
            sp.dma_start(rope_sb[:, :, :], rope).then_inc(s_c, 16)
            sp.dma_start(acc[:, TJ:2 * TJ, :], x_v[:, 1]).then_inc(s_x[1], 16)
            sp.dma_start(vb_sb[:, :], vb.partition_broadcast(P)).then_inc(s_c, 16)
            sp.dma_start(ob_sb[:, :], ob.partition_broadcast(P)).then_inc(s_c, 16)
            sp.dma_start(wo_sb[:, :], wo).then_inc(s_c, 16)
            sp.dma_start(gw_sb[:, :], gw).then_inc(s_c, 16)
            for b in range(2, NB):
                sp.dma_start(acc[:, TJ * b:TJ * b + TJ, :], x_v[:, b]).then_inc(s_x[b], 16)

            def load_xTb(b):
                p = b.n % 2
                wait(sp, s_xnT, b.at(b.n + 1, 1))
                wait(sp, v_ready, b.at(b.n - 1, 1))
                col = b.at(b.n * S, S)
                src = xnT[:, col:col + S] if isinstance(col, int) else xnT[:, bass.ds(col, S)]
                sp.dma_start(xTb[p][:, :], src).then_inc(xtb[p], 16)

            def stack(b, i):
                p = b.n % 2
                wait(sp, st_full, b.at(UNITS * (NI * (b.n - 2) + i + 1), UNITS * NI))
                wait(sp, split, b.at(2 * b.n + 2, 2))
                wait(sp, stacked[i], b.at(PIECES * b.n, PIECES))
                src = slice(32 * i, 32 * i + 32)
                both = stacks[p][:, :, i, :]
                for dst, what in ((both[0:P:4, 0], halves[src, 2]), (both[0:P:4, 1], halves[src, 1]),
                                  (both[1:P:4], halves[src, 2:4]), (both[2:P:4], halves[src, 0:2]),
                                  (both[3:P:4, 0], zeros[:, :])):
                    sp.dma_start(dst.bitcast(F32), what.bitcast(F32)).then_inc(stacked[i], 16)

            def put_mrows(b, i):
                wait(sp, mrow_done, b.at(NI * b.n + i + 1, NI))
                sp.dma_start(m_dram[i].rearrange("r (g j) t -> (g j) r t", g=G),
                             mrow[i][:, :, :].bitcast(F32)).then_inc(mstored, 16)
                sp.wait_ge(mstored, b.at(16 * (NI * b.n + i + 1), 16 * NI))
                wait(sp, mrows[i], b.at(32 * b.n, 32))
                sp.wait_ge(stacked[i], b.at(PIECES * (b.n + 1), PIECES))
                for r in range(2):
                    sp.dma_start(stack_q[b.n % 2][3 + 4 * r:P:32, i, :].bitcast(F32),
                                 m_dram[i, r].rearrange("(g j) t -> g (j t)", g=G)).then_inc(mrows[i], 16)

            sp.wait_ge(s_zero, 1)
            sp.wait_ge(s_ones, 2)
            load_xTb(Batch(0))
            load_xTb(Batch(1))
            for i in range(NI):
                stack(Batch(0), i)
            for i in range(NI):
                stack(Batch(1), i)
            load_xTb(Batch(2))
            for i in range(NI - 1):
                put_mrows(Batch(0), i)

            def step(b):
                for i in range(NI):
                    if i == 0:
                        put_mrows(b, NI - 1)
                    elif b.n + 1 < NB:
                        put_mrows(b.plus(1), i - 1)
                    if b.n + 2 < NB:
                        stack(b.plus(2), i)
                if b.n + 3 < NB:
                    load_xTb(b.plus(3))

            loops(sp, step)
            sp.wait_ge(acc_done, NB)

        @block.gpsimd
        def _(pool):
            for t in stack_k:
                nc.gpsimd.memset(t.bitcast(F32), 1.0).then_inc(s_ones, 1)
            nc.gpsimd.memset(zeros[:, :].bitcast(F32), 0.0).then_inc(s_zero, 1)
            nc.gpsimd.memset(ident[:, :], 0.0).then_inc(s_pc, 1)
            nc.gpsimd.memset(maskb[:, :, :], 0.0).then_inc(s_pc, 1)
            nc.gpsimd.memset(half[:, :], -0.5).then_inc(s_pc, 1)
            pool.wait_ge(s_pc, 3)
            nc.gpsimd.affine_select(out=ident[:, :], in_=ident[:, :], pattern=[[-1, P]], compare_op=ALU.not_equal,
                                    fill=1.0, base=0, channel_multiplier=1).then_inc(s_pc, 1)
            nc.gpsimd.affine_select(out=maskb[:, :, :], in_=maskb[:, :, :], pattern=[[0, 2], [-1, P]],
                                    compare_op=ALU.is_ge, fill=NEG, base=0, channel_multiplier=1).then_inc(s_pc, 1)
            pool.wait_ge(s_pc, 5)
            nc.gpsimd.tensor_copy(identb[:, :], ident[:, :]).then_inc(s_consts, 1)
            for b in range(NB):
                pool.wait_ge(s_eps, b + 1)
                nc.gpsimd.tensor_tensor(rstd[:, TJ * b:TJ * b + TJ], rstd[:, TJ * b:TJ * b + TJ], half[:, :],
                                        ALU.pow).then_inc(s_rstd, 1)
            pool.wait_ge(s_c, N_CONST)

            def rope_qk(b, k):
                wait(pool, ev_done, b.at(4 * b.n + 2 * k + 2, 4))
                wait(pool, split, b.at(2 * b.n, 2))
                a_, b_ = ev[:, 2 * k], ev[:, 2 * k + 1]
                chain = b.at(6 * b.n + 3 * k, 6)
                nc.gpsimd.tensor_tensor(a_, a_, rope_sb[:, 0], ALU.mult).then_inc(s_rp, 1)
                nc.gpsimd.tensor_tensor(b_, b_, rope_sb[:, 1], ALU.mult).then_inc(s_rp, 1)
                pool.wait_ge(s_rp, b.at(4 * b.n + 2 * k + 2, 4))
                nc.gpsimd.tensor_tensor(qk[:, k], a_, b_, ALU.add).then_inc(roped, 1)

            for b in range(2):
                rope_qk(Batch(b), 0)
                rope_qk(Batch(b), 1)
            for b in range(NB):
                pool.wait_ge(s_xn, TJ * (b + 1))
                t = acc[:, TJ * b:TJ * b + TJ, :]
                nc.gpsimd.tensor_tensor(t, t, ob_sb[:, :].unsqueeze(1).to_broadcast([P, TJ, D]), ALU.add).then_inc(s_xr, 1)

            def step(b):
                for i in range(NI):
                    gpar = i % 2
                    for u in range(PAIRS):
                        c, gp = u % 3, u // 3
                        pool.wait_ge(exp_done, b.at(UNITS * (NI * b.n + i) + 2 * u + 2, UNITS * NI))
                        at = CHUNK_AT[c]
                        if c < 2:
                            v = probs[gpar][:, 2 * gp:2 * gp + 2, at:at + P]
                            pat = [[0, 2], [1, P]]
                            nc.gpsimd.affine_select(out=v, in_=v, pattern=pat, compare_op=ALU.is_ge, fill=0.0,
                                                    base=0, channel_multiplier=-1).then_inc(masked, 1)
                        else:
                            for k in range(2):
                                v = probs[gpar][:, 2 * gp:2 * gp + 2, at + 256 * k:at + 256 * k + P]
                                last = nc.gpsimd.affine_select(out=v, in_=v, pattern=[[0, 2], [1, P]],
                                                               compare_op=ALU.is_ge, fill=0.0, base=0,
                                                               channel_multiplier=-1)
                                last.then_inc(masked, 1)
                        if u == 2 and i in (1, 2) and b.n + 2 < NB:
                            rope_qk(b.plus(2), i - 1)

            loops(pool, step)

        @block.scalar
        def _(act):
            def evac_qk(b, k, where=None):
                key = ("QQ", "KK")[k]
                wait(act, roped, b.at(2 * (b.n - 1) + k + 1, 2))
                w, n = slot((key, b.n) if where else key, b if where else b.plus(-2), where)
                act.wait_ge(wk_full[w], n)
                for h in range(2):
                    m = 2 * k + h
                    nc.scalar.activation(ev[:, m], wk[:, w, h, :], ACT.Identity, bias=qkb_sb[:, m:m + 1]).then_inc(ev_done, 1)
                act.wait_ge(ev_done, b.at(4 * b.n + 2 * k + 2, 4))
                act.sem_inc(wk_free[w], 1)

            def evac_plain(key, b, where, dst, done, count):
                w, n = slot(key, b, where)
                act.wait_ge(wk_full[w], n)
                nc.scalar.activation(dst, wk[:, w, 0, :], ACT.Copy).then_inc(done, 1)
                act.wait_ge(done, count)
                act.sem_inc(wk_free[w], 1)

            act.wait_ge(s_c, N_CONST)
            for b in range(2):
                evac_plain(("XT", b), None, "pro", xnT[:, S * b:S * b + S], s_xnT, b + 1)
            for b in range(2):
                evac_qk(Batch(b), 0, "pro")
                evac_qk(Batch(b), 1, "pro")
            for b in range(2, NB):
                evac_plain(("XT", b), None, "pro", xnT[:, S * b:S * b + S], s_xnT, b + 1)

            def evac_o(b, i):
                act.wait_ge(pv_done, b.at(NI * b.n + i + 1, NI))
                wait(act, s_nt, b.at(NI * b.n + i - 1, NI))
                nc.scalar.activation(o_sb[i % 2][:, :], po[:, :], ACT.Copy).then_inc(o_evac, 1)

            def evac_at(b, key_b, where):
                wait(act, s_op, b.at(b.n, 1))
                evac_plain("AT", key_b, where, attnT[:, :], attnT_done, b.at(b.n + 1, 1))

            def exps(b, i, pair):
                gp, c = divmod(pair, 3)
                group = NI * b.n + i
                if pair == 0:
                    wait(act, pv_done, b.at(group - 1, NI))
                at, w = CHUNK_AT[c], CHUNK_W[c]
                for h in range(2):
                    n = UNITS * group + 2 * pair + h
                    act.wait_ge(st_full, b.at(n + 1, UNITS * NI))
                    nc.scalar.activation(probs[i % 2][:, 2 * gp + h, at:at + w], st[:, n % ST_BANKS, 0:w],
                                         ACT.Exp, scale=SCALE).then_inc(exp_done, 1)

            def step(b):
                most = b.n + 2 < NB
                for i in range(NI):
                    exps(b, i, 0)
                    exps(b, i, 1)
                    exps(b, i, 2)
                    exps(b, i, 3)
                    if i > 0 or b.n > 0:
                        evac_o(b if i else b.plus(-1), (i - 1) % NI)
                    exps(b, i, 4)
                    if i < 2 and most:
                        evac_qk(b.plus(2), i)
                    if i == 2 and b.n > 0:
                        evac_at(b.plus(-1), b, None)
                    exps(b, i, 5)

            loops(act, step)
            evac_o(Batch(NB - 1), NI - 1)
            evac_at(Batch(NB - 1), None, "epi")


        @block.vector
        def _(dve):
            chain = [0]

            def link(ins):
                chain[0] += 1
                ins.then_inc(s_chain, 1)
                dve.wait_ge(s_chain, chain[0])

            for t in v32:
                nc.vector.memset(t[:, :, :, :], 0.0).then_inc(s_vz, 1)
            dve.wait_ge(s_vz, 2)
            for t in v32:
                nc.vector.memset(t[:, :, :, HD:HD + 1], 1.0).then_inc(s_vz, 1)
            for b in range(NB):
                dve.wait_ge(s_x[b], 16)
                for j in range(TJ):
                    t = TJ * b + j
                    nc.vector.bn_stats(stats[:, t, :], acc[:, t, :]).then_inc(s_stat, 1)
                dve.wait_ge(s_stat, TJ * (b + 1))
                for j in range(TJ):
                    t = TJ * b + j
                    nc.vector.bn_aggr(mv[:, t, :], stats[:, t, :]).then_inc(s_mv, 1)
                dve.wait_ge(s_mv, TJ * (b + 1))
                nc.vector.tensor_scalar_add(rstd[:, TJ * b:TJ * b + TJ], mv[:, TJ * b:TJ * b + TJ, 1],
                                            EPS).then_inc(s_eps, 1)
                dve.wait_ge(s_rstd, b + 1)
                for j in range(TJ):
                    t = TJ * b + j
                    nc.vector.tensor_scalar(xn[:, t, :], acc[:, t, :], mv[:, t, 0:1], rstd[:, t:t + 1],
                                            ALU.subtract, ALU.mult).then_inc(s_xn, 1)
                if b == 1:
                    pass

            def split_qk(b, k):
                dve.wait_ge(roped, b.at(2 * b.n + k + 1, 2))
                for p in range(NI):
                    wait(dve, stacked[p], b.at(PIECES * b.n, PIECES))
                nc.vector.tensor_copy(high[k], qk[:, k]).then_inc(s_hi, 1)
                dve.wait_ge(s_hi, b.at(2 * b.n + k + 1, 2))
                nc.vector.tensor_tensor(low[k], qk[:, k], high[k].bitcast(F32), ALU.subtract).then_inc(split, 1)

            def put_v(b, key, key_b, where):
                bank, n = slot(key, key_b, where)
                dve.wait_ge(wk_full[bank], n)
                wait(dve, pv_done, b.at(NI * (b.n - 1), NI))
                src = wk[:, bank, 0, :].rearrange("p (j h d) -> p j h d", j=TJ, h=H)
                bias = vb_sb[:, :].rearrange("p (h d) -> p h d", h=H).unsqueeze(1).to_broadcast([P, TJ, H, HD])
                nc.vector.tensor_tensor(v32[b.n % 2][:, :, :, 0:HD], src, bias, ALU.add).then_inc(v_ready, 1)
                dve.wait_ge(v_ready, b.at(b.n + 1, 1))
                dve.sem_inc(wk_free[bank], 1)

            def maxima(b, key_b, i, pair, where=None, turns=False):
                gp, c = divmod(pair, 3)
                if pair == 0:
                    wait(dve, s_mt, b.at(NI * b.n + i - 1, NI))
                w, n = slot(("S", i, pair), key_b, where)
                dve.wait_ge(wk_full[w], n)
                g = slice(2 * gp, 2 * gp + 2)
                if c == 0:
                    dst, src = part[i % 2][:, g, :], wk[:, w, :, 0:3 * P].rearrange("p h (u k) -> p h u k", u=3)
                else:
                    dst, src = nm[i % 2][:, g, c + 1], wk[:, w, :, 0:(c + 2) * P]
                if turns:
                    nc.vector.tensor_reduce(dst, src, AX.X, ALU.max, negate=True).then_inc(s_red, 1)
                else:
                    nc.vector.tensor_reduce(dst, src, AX.X, ALU.max, negate=True).then_inc(wk_free[w], 1)
                if pair == 5:
                    dve.wait_ge(wk_free[w], n)
                    nc.vector.tensor_copy(nm[i % 2][:, :, 0], part[i % 2][:, :, 0]).then_inc(nm_done, 1)
                    nc.vector.tensor_tensor(nm[i % 2][:, :, 1], part[i % 2][:, :, 1], part[i % 2][:, :, 2],
                                            ALU.min).then_inc(nm_done, 1)

            def max_rows(b, key, key_b, i, where):
                w, n = slot(key, key_b, where)
                dve.wait_ge(wk_full[w], n)
                wait(dve, mrows[i], b.at(32 * b.n, 32))
                src = wk[0:G * TJ, w, 0, 3 * P:4 * P]
                nc.vector.tensor_copy(mrow[i][:, 0, :], src).then_inc(s_mh, 1)
                dve.wait_ge(s_mh, b.at(NI * b.n + i + 1, NI))
                nc.vector.tensor_tensor(mrow[i][:, 1, :], src, mrow[i][:, 0, :].bitcast(F32),
                                        ALU.subtract).then_inc(mrow_done, 1)
                dve.wait_ge(mrow_done, b.at(NI * b.n + i + 1, NI))
                dve.sem_inc(wk_free[w], 1)

            def norm(b, key, key_b, i, where=None):
                bank, n = slot(key, key_b, where)
                dve.wait_ge(wk_full[bank], n)
                src = wk[:, bank, 0, :].rearrange("p (j g c) -> p j g c", j=TJ, g=G)
                nc.vector.reciprocal(rec[:, :, :], src[:, :, :, HD]).then_inc(s_rec, 1)
                dve.wait_ge(s_rec, b.at(NI * b.n + i + 1, NI))
                if i == 0:
                    wait(dve, s_at, b.at(b.n - 1, 1))
                dst = attn[b.n % 2][:, :, 32 * i:32 * i + 32].rearrange("p j (g d) -> p j g d", g=G)
                nc.vector.tensor_tensor(dst, src[:, :, :, 0:HD], rec[:, :, :].unsqueeze(3).to_broadcast([P, TJ, G, HD]),
                                        ALU.mult).then_inc(attn_done, 1)
                dve.wait_ge(attn_done, b.at(NI * b.n + i + 1, NI))
                dve.sem_inc(wk_free[bank], 1)

            def add_out(b, key_b, where=None):
                bank, n = slot("OP", key_b, where)
                dve.wait_ge(wk_full[bank], n)
                row = b.at(TJ * b.n, TJ)
                t = acc[:, row:row + TJ, :] if isinstance(row, int) else acc[:, bass.ds(row, TJ), :]
                nc.vector.tensor_tensor(t, wk[:, bank, 0, :].rearrange("p (j d) -> p j d", j=TJ), t,
                                        ALU.add).then_inc(acc_done, 1)
                dve.wait_ge(acc_done, b.at(b.n + 1, 1))
                dve.sem_inc(wk_free[bank], 1)

            b0, b1 = Batch(0), Batch(1)
            split_qk(b0, 0)
            split_qk(b0, 1)
            put_v(b0, ("V", 0), None, "pro")
            split_qk(b1, 0)
            split_qk(b1, 1)
            bank, n = slot("GT", None, "pro")
            dve.wait_ge(wk_full[bank], n)
            nc.vector.tensor_copy(logits[:, :, :], wk[:, bank, 0, 0:NT * E].rearrange("p (t e) -> p t e", e=E)).then_inc(wk_free[bank], 1)
            dve.wait_ge(wk_free[bank], n)
            dve.wait_ge(s_xr, NB)
            for i in range(NI):
                for pair in range(PAIRS):
                    turns = pair == 1 and i > 0
                    maxima(b0, None, i, pair, "pro", turns)
                    if turns:
                        dve.wait_ge(s_red, i)
                        max_rows(b0, ("S", i, 1), None, i - 1, "pro")

            def step(b):
                more, most = b.n + 1 < NB, b.n + 2 < NB
                for i in range(NI):
                    for pair in range(PAIRS):
                        if more:
                            maxima(b.plus(1), b, i, pair, None, pair == 1)
                        if pair == 1 and more:
                            dve.wait_ge(s_red, b.at(NI * b.n + i + NI, NI))
                        if pair == 1 and (more or i == 0):
                            max_rows(b if i == 0 else b.plus(1), ("S", i, 1), b, (i - 1) % NI, None)
                        if pair == 3 and i == 3 and b.n > 0:
                            add_out(b.plus(-1), b)
                        if pair == 4 and (i > 0 or b.n > 0):
                            norm(b if i else b.plus(-1), ("N", i), b, (i - 1) % NI)
                    if i == 1 and most:
                        split_qk(b.plus(2), 0)
                    if i == 2 and most:
                        split_qk(b.plus(2), 1)
                    if i == 3 and more:
                        put_v(b.plus(1), "V", b, None)

            loops(dve, step)
            norm(Batch(NB - 1), "N", None, NI - 1, "epi")
            add_out(Batch(NB - 1), None, "epi")


        @block.tensor
        def _(pe):
            def fill(key, b, where=None):
                bank, n = slot(key, b, where)
                wait(pe, wk_free[bank], n - 1)
                return bank

            def scores(b, key_b, i, pair, where=None, turns=None):
                gp, c = divmod(pair, 3)
                q, k = stack_q[b.n % 2], stack_k[b.n % 2]
                w = fill(("S", i, pair), key_b, where)
                if turns is not None:
                    of, ti = turns
                    pe.wait_ge(nm_done, of.at(2 * (NI * of.n + ti + 1), 2 * NI))
                    nc.tensor.matmul(wk[0:G * TJ, w, 0, 3 * P:4 * P], nm[ti % 2][:, :, :].rearrange("p g j -> p (g j)"),
                                     ident[:, :], start=True, stop=True, skip_group_check=True).then_inc(s_mt, 1)
                if b.n >= NB:
                    pe.wait_ge(s_mt, of.at(NI * of.n + ti + 1, NI))
                    pe.sem_inc(wk_full[w], 1)
                    return
                for at, j in ([(0, 0), (P, 1)] if c == 0 else [(0, c + 1)]):
                    for h in range(2):
                        g = 2 * gp + h
                        r, width = slice(32 * g, 32 * g + 32), (j + 1) * P
                        nc.tensor.matmul(wk[:, w, h, at:at + width], q[r, i, j * P:j * P + P], k[r, i, 0:width],
                                         start=at == 0, stop=False, skip_group_check=True)
                for h in range(2):
                    if c == 0:
                        diag, mask = wk[:, w, h, :].rearrange("p (a t) -> p a t", a=2)[:, :, 0:P], maskb[:, :, :]
                    else:
                        diag, mask = wk[:, w, h, (c + 1) * P:(c + 2) * P], maskb[:, 0, :]
                    last = nc.tensor.matmul(diag, identb[:, :], mask, start=False, stop=True, skip_group_check=True)
                last.then_inc(wk_full[w], 1)

            def scores_t(b, i, pair):
                gp, c = divmod(pair, 3)
                n = UNITS * (NI * b.n + i) + 2 * pair
                if pair == 0:
                    pe.wait_ge(mrows[i], b.at(32 * (b.n + 1), 32))
                wait(pe, exp_done, b.at(n + 2 - ST_BANKS, UNITS * NI))
                q, k = stack_q[b.n % 2], stack_k[b.n % 2]
                for at, kt, w in CHUNKS[c]:
                    for h in range(2):
                        g = 2 * gp + h
                        r = slice(32 * g, 32 * g + 32)
                        last = nc.tensor.matmul(st[:, (n + h) % ST_BANKS, at:at + w], k[r, i, kt * P:kt * P + P],
                                                q[r, i, kt * P:S], start=True, stop=True, skip_group_check=True)
                        if at + w == CHUNK_W[c]:
                            last.then_inc(st_full, 1)

            def weigh(b, i, tiles):
                if 0 in tiles:
                    pe.wait_ge(masked, b.at(8 * (NI * b.n + i + 1), 8 * NI))
                    if i == 0:
                        pe.wait_ge(v_ready, b.at(b.n + 1, 1))
                    wait(pe, o_evac, b.at(NI * b.n + i, NI))
                for c in range(3):
                    for at, kt, w in CHUNKS[c]:
                        if kt in tiles:
                            for g in range(G):
                                o = CHUNK_AT[c] + at
                                last = nc.tensor.matmul(po[32 * g:32 * g + 32, kt * P:S], v32[b.n % 2][:, kt, 4 * i + g, :],
                                                        probs[i % 2][:, g, o:o + w], start=kt == 0, stop=kt == TJ - 1,
                                                        skip_group_check=True)
                if TJ - 1 in tiles:
                    last.then_inc(pv_done, 1)

            def turn_o(b, key, key_b, i, where=None):
                pe.wait_ge(o_evac, b.at(NI * b.n + i + 1, NI))
                bank = fill(key, key_b, where)
                for j in range(TJ):
                    last = nc.tensor.transpose(wk[:, bank, 0, j * P:j * P + P], o_sb[i % 2][:, j * P:j * P + P], ident[:, :])
                last.then_inc(wk_full[bank], 1)
                pe.wait_ge(wk_full[bank], slot(key, key_b, where)[1])
                pe.sem_inc(s_nt, 1)

            def project(b, k, h, key, key_b, where=None):
                pe.wait_ge(xtb[b.n % 2], b.at(16 * (b.n // 2 + 1), 8))
                w = fill(key, key_b, where)
                m = 2 * k + h
                last = nc.tensor.matmul(wk[:, w, h, :], w_sb[:, m * D:m * D + D], xTb[b.n % 2][:, :], start=True, stop=True)
                if h == 1:
                    last.then_inc(wk_full[w], 1)

            def project_v(b, key, key_b, where=None):
                pe.wait_ge(xtb[b.n % 2], b.at(16 * (b.n // 2 + 1), 8))
                bank = fill(key, key_b, where)
                for j in range(TJ):
                    last = nc.tensor.matmul(wk[:, bank, 0, j * D:j * D + D], xTb[b.n % 2][:, j * P:j * P + P],
                                            w_sb[:, 4 * D:5 * D], start=True, stop=True)
                last.then_inc(wk_full[bank], 1)

            def turn_attn(b, key_b, where=None):
                pe.wait_ge(attn_done, b.at(NI * (b.n + 1), NI))
                bank = fill("AT", key_b, where)
                for j in range(TJ):
                    last = nc.tensor.transpose(wk[:, bank, 0, j * P:j * P + P], attn[b.n % 2][:, j, :], ident[:, :])
                last.then_inc(wk_full[bank], 1)
                pe.wait_ge(wk_full[bank], slot("AT", key_b, where)[1])
                pe.sem_inc(s_at, 1)

            def project_out(b, key_b, where=None):
                pe.wait_ge(attnT_done, b.at(b.n + 1, 1))
                bank = fill("OP", key_b, where)
                for j in range(TJ):
                    last = nc.tensor.matmul(wk[:, bank, 0, j * D:j * D + D], attnT[:, j * P:j * P + P], wo_sb[:, :],
                                            start=True, stop=True)
                last.then_inc(wk_full[bank], 1)
                pe.wait_ge(wk_full[bank], slot("OP", key_b, where)[1])
                pe.sem_inc(s_op, 1)

            def turn_x(b):
                pe.wait_ge(s_xn, TJ * (b + 1))
                bank = fill(("XT", b), None, "pro")
                for j in range(TJ):
                    last = nc.tensor.transpose(wk[:, bank, 0, j * P:j * P + P], xn[:, TJ * b + j, :], ident[:, :])
                last.then_inc(wk_full[bank], 1)

            pe.wait_ge(s_consts, 1)
            turn_x(0)
            turn_x(1)
            pe.wait_ge(s_c, N_CONST)
            for b in (Batch(0), Batch(1)):
                for k, name in enumerate(("QQ", "KK")):
                    project(b, k, 0, (name, b.n), None, "pro")
                    project(b, k, 1, (name, b.n), None, "pro")
                if b.n == 0:
                    project_v(b, ("V", 0), None, "pro")
            for b in range(2, NB):
                turn_x(b)
            bank = fill("GT", None, "pro")
            pe.wait_ge(s_xnT, NB)
            for t in range(NT):
                last = nc.tensor.matmul(wk[:, bank, 0, t * E:t * E + E], xnT[:, t * P:t * P + P], gw_sb[:, :],
                                        start=True, stop=True)
            last.then_inc(wk_full[bank], 1)
            pe.wait_ge(s_ones, 2)

            def wait_stack(b, i):
                pe.wait_ge(stacked[i], b.at(PIECES * (b.n + 1), PIECES))

            for i in range(NI):
                wait_stack(Batch(0), i)
                for pair in range(PAIRS):
                    scores(Batch(0), None, i, pair, "pro", (Batch(0), i - 1) if pair == 1 and i > 0 else None)

            def step(b):
                more, most = b.n + 1 < NB, b.n + 2 < NB
                b1, b2 = b.plus(1), b.plus(2)
                for i in range(NI):
                    prev, weighs = (b if i else b.plus(-1)), i > 0 or b.n > 0
                    if more:
                        wait_stack(b1, i)
                    for pair in range(PAIRS):
                        scores_t(b, i, pair)
                        turned = (b if i == 0 else b1, (i - 1) % NI) if pair == 1 else None
                        if more or pair == 1 and i == 0:
                            scores(b1, b, i, pair, None, turned)
                        if pair == 1 and weighs:
                            weigh(prev, (i - 1) % NI, (0,))
                        if pair == 2 and weighs:
                            weigh(prev, (i - 1) % NI, (1,))
                        if pair == 3 and weighs:
                            weigh(prev, (i - 1) % NI, (2, 3))
                        if pair == 3:
                            if i < 2 and most:
                                project(b2, i, 0, ("QQ", "KK")[i], b)
                            if i == 2 and b.n > 0:
                                turn_attn(b.plus(-1), b)
                            if i == 3 and b.n > 0:
                                project_out(b.plus(-1), b)
                        if pair == 4:
                            if i < 2 and most:
                                project(b2, i, 1, ("QQ", "KK")[i], b)
                            if weighs:
                                turn_o(prev, ("N", i), b, (i - 1) % NI)
                        if pair == 5 and i == 3 and more:
                            project_v(b1, "V", b)

            loops(pe, step)
            weigh(Batch(NB - 1), NI - 1, range(TJ))
            turn_o(Batch(NB - 1), "N", None, NI - 1, "epi")
            turn_attn(Batch(NB - 1), None, "epi")
            project_out(Batch(NB - 1), None, "epi")


def experts(nc, w1, w2, b2, route, acc, xn, logits, ident, out):
    ctx = ExitStack()
    with ctx:
        def sb(name, shape, dt=F32):
            return ctx.enter_context(nc.sbuf_tensor(name, shape, dt))

        def sem(name):
            return ctx.enter_context(nc.semaphore(name))

        U32, I32 = mybir.dt.uint32, mybir.dt.int32
        w1_sb = sb("w1_sb", [P, E, F + FC])
        w2_sb = sb("w2_sb", [P, E, F + D])
        w1_e = [sb(f"w1_e{p}", [P, F + FC]) for p in range(2)]
        w2_e = [sb(f"w2_e{p}", [P, F + D]) for p in range(2)]
        table = sb("table", [P, E + BLOCKS + 2 * P])
        prefer, number = table[:, 0:E], table[:, E:E + BLOCKS]
        ones, above = table[:, E + BLOCKS:E + BLOCKS + P], table[:, E + BLOCKS + P:]
        chosen = sb("chosen", [P, 2, NT, E])
        lower = sb("lower", [P, NT, E])
        tmp = sb("tmp", [P, NT, E])
        best = sb("best", [P, 2, NT])
        lead = sb("lead", [P, NT])
        either = sb("either", [P, NT, E])
        sums = [sb(f"sums{p}", [P, NT, E]) for p in range(2)]
        share = sb("share", [P, 2, NT])
        blocks_i = sb("blocks_i", [P, E], I32)
        ends = [sb(f"ends{p}", [P, E]) for p in range(2)]
        starts = sb("starts", [P, E])
        beyond = sb("beyond", [P, BLOCKS, E])
        expert_f = sb("expert_f", [P, BLOCKS])
        expert = sb("expert", [P, BLOCKS], I32)
        place_f = sb("place_f", [P, 2, NT])
        place = sb("place", [P, 2, NT], U32)
        blank = sb("blank", [P, 9, D])
        xg = [sb(f"xg{p}", [P, D]) for p in range(TURN)]
        xgT = [sb(f"xgT{p}", [P, P]) for p in range(2)]
        h = [sb(f"h{p}", [P, FC, P]) for p in range(2)]
        y = [sb(f"y{p}", [P, D]) for p in range(TURN)]
        YB = 4
        yg = sb("yg", [P, YB, D])

        count_ps = ctx.enter_context(nc.psum_tensor("count_ps", [P, 2, 256], F32))
        xT_ps = ctx.enter_context(nc.psum_tensor("xT_ps", [P, 2, 512], F32))
        h_ps = ctx.enter_context(nc.psum_tensor("h_ps", [P, 2, 512], F32))
        y_ps = ctx.enter_context(nc.psum_tensor("y_ps", [P, 2, 512], F32))
        xg_dram = nc.dram_tensor("xg_dram", (BLOCKS * P, D), F32, kind="Internal").ap()
        y_dram = nc.dram_tensor("y_dram", (BLOCKS * P, D), F32, kind="Internal").ap()
        out_v = out.rearrange("b (j p) d -> p (b j) d", p=P)

        f_loaded = sem("f_loaded")
        f_blank = sem("f_blank")
        f_blanked = sem("f_blanked")
        f_route = sem("f_route")
        f_either = sem("f_either")
        f_counted = sem("f_counted")
        f_lead = sem("f_lead")
        f_exp = sem("f_exp")
        f_placed = sem("f_placed")
        f_experts = sem("f_experts")
        f_scattered = sem("f_scattered")
        f_xg = [sem(f"f_xg{p}") for p in range(TURN)]
        f_w1 = sem("f_w1")
        f_w2 = sem("f_w2")
        f_xT = sem("f_xT")
        f_xTs = sem("f_xTs")
        f_up = sem("f_up")
        f_gelu = sem("f_gelu")
        f_down = sem("f_down")
        f_y = sem("f_y")
        f_ys = [sem(f"f_ys{p}") for p in range(TURN)]
        f_yg = [sem(f"f_yg{k}") for k in range(YB)]
        f_sum = sem("f_sum")
        f_out = sem("f_out")

        def wait(eng, s, v):
            if not (isinstance(v, int) and v <= 0):
                eng.wait_ge(s, v)

        block = ctx.enter_context(nc.Block())

        class Block:
            def __init__(self, n, turn=None):
                self.n, self.turn, self.p, self.q = n, turn, n % 2, n % TURN

            def plus(self, v):
                return self.times(1, v)

            def times(self, v, c=0):
                return self.n * v + c if self.turn is None else self.turn * (TURN * v) + (self.n * v + c)

            def landed(self, c=0):
                v = 16 * (self.n // TURN + 1 + c)
                return v if self.turn is None else self.turn * 16 + v

            def later(self, v):
                return Block(self.n + v, self.turn)

        def blocks(eng, body, ahead):
            for n in range(TURN):
                body(Block(n), True)
            with eng.Fori(1, BLOCKS // TURN - 1) as turn:
                for n in range(TURN):
                    body(Block(n, turn), True)
            for n in range(BLOCKS - TURN, BLOCKS):
                body(Block(n), n + ahead < BLOCKS)

        def expert_of(eng, k):
            at = k.plus(0)
            return eng.value_load(expert[0:1, at:at + 1] if isinstance(at, int) else expert[0:1, bass.ds(at, 1)],
                                  min_val=0, max_val=E - 1)

        @block.sync
        def _(sp):
            sp.dma_start(table[:, :], route).then_inc(f_loaded, 16)
            sp.dma_start(w1_sb[:, :, :], w1).then_inc(f_loaded, 16)
            sp.dma_start(w2_sb[:, :, 0:F], w2).then_inc(f_loaded, 16)
            sp.dma_start(w2_sb[:, :, F:], b2.partition_broadcast(P)).then_inc(f_loaded, 16)
            sp.wait_ge(f_blank, 1)
            for k in range(0, BLOCKS, 9):
                n = min(9, BLOCKS - k)
                sp.dma_start(xg_dram[k * P:(k + n) * P, :].rearrange("(k p) d -> p k d", p=P),
                             blank[:, 0:n, :]).then_inc(f_blanked, 16)
            sp.wait_ge(f_scattered, 16 * 2 * NT)

            def load(k):
                wait(sp, f_xT, k.plus(1 - TURN))
                at = k.times(P)
                src = xg_dram[at:at + P, :] if isinstance(at, int) else xg_dram[bass.ds(at, P), :]
                sp.dma_start(xg[k.q][:, :], src).then_inc(f_xg[k.q], 16)

            def store(k):
                sp.wait_ge(f_y, k.plus(1))
                at = k.times(P)
                dst = y_dram[at:at + P, :] if isinstance(at, int) else y_dram[bass.ds(at, P), :]
                sp.dma_start(dst, y[k.q][:, :]).then_inc(f_ys[k.q], 16)

            for n in range(TURN):
                load(Block(n))

            def step(k, more):
                store(k)
                if more:
                    load(k.later(TURN))

            blocks(sp, step, TURN)
            sp.wait_ge(f_sum, 2 * NT)
            sp.dma_start(out_v, acc[:, :, :]).then_inc(f_out, 16)
            sp.wait_ge(f_out, 16)

        @block.gpsimd
        def _(pool):
            nc.gpsimd.memset(blank[:, :, :], 0.0).then_inc(f_blank, 1)
            pool.wait_ge(f_placed, 1)
            pool.wait_ge(f_blanked, 16 * (-(-BLOCKS // 9)))
            for t in range(NT):
                for c in range(2):
                    nc.gpsimd.indirect_dma_start(xg_dram[:, :], bass.IndirectOffsetOnAxis(place[:, c, t:t + 1], 0),
                                                 xn[:, t, :], None).then_inc(f_scattered, 16)
            for p in range(TURN):
                pool.wait_ge(f_ys[p], 16 * (BLOCKS // TURN))
            for n in range(2 * NT):
                t, c = divmod(n, 2)
                wait(pool, f_sum, n - YB + 1)
                nc.gpsimd.indirect_dma_start(yg[:, n % YB, :], None, y_dram[:, :],
                                             bass.IndirectOffsetOnAxis(place[:, c, t:t + 1], 0)).then_inc(f_yg[n % YB], 16)

        @block.scalar
        def _(act):
            act.wait_ge(f_lead, 1)
            nc.scalar.activation(lead[:, :], lead[:, :], ACT.Exp).then_inc(f_exp, 1)

            def gelu(k, _):
                act.wait_ge(f_up, k.plus(1))
                act.wait_ge(f_w1, k.plus(1))
                wait(act, f_down, k.plus(-1))
                for c in range(FC):
                    last = nc.scalar.activation(h[k.p][:, c, :], h_ps[:, k.p, c * P:c * P + P], ACT.Gelu,
                                                bias=w1_e[k.p][:, F + c:F + c + 1])
                last.then_inc(f_gelu, 1)

            blocks(act, gelu, 0)

        @block.vector
        def _(dve):
            links = [0]

            def link(ins):
                links[0] += 1
                ins.then_inc(f_route, 1)
                dve.wait_ge(f_route, links[0])

            def along_e(v):
                return v.unsqueeze(2).to_broadcast([P, NT, E])

            prefers = prefer.unsqueeze(1).to_broadcast([P, NT, E])
            dve.wait_ge(f_loaded, 4 * 16)
            scores = logits
            for c in range(2):
                link(nc.vector.tensor_reduce(best[:, c], scores[:, :, :], AX.X, ALU.max))
                link(nc.vector.tensor_tensor(tmp[:, :, :], scores[:, :, :], along_e(best[:, c]), ALU.is_equal))
                link(nc.vector.tensor_tensor(tmp[:, :, :], tmp[:, :, :], prefers, ALU.mult))
                link(nc.vector.tensor_reduce(share[:, c], tmp[:, :, :], AX.X, ALU.max))
                link(nc.vector.tensor_tensor(chosen[:, c], prefers, along_e(share[:, c]), ALU.is_equal))
                if c == 0:
                    link(nc.vector.scalar_tensor_tensor(lower[:, :, :], chosen[:, 0], -3e38, logits[:, :, :],
                                                        ALU.mult, ALU.add))
                    scores = lower
            nc.vector.tensor_tensor(either[:, :, :], chosen[:, 0], chosen[:, 1], ALU.add).then_inc(f_either, 1)
            nc.vector.tensor_tensor(lead[:, :], best[:, 1], best[:, 0], ALU.subtract).then_inc(f_lead, 1)
            dve.wait_ge(f_counted, 1)
            link(nc.vector.tensor_copy(sums[0][:, :, :], count_ps[:, 0, :].rearrange("p (t e) -> p t e", e=E)))
            a, step = 0, 1
            while step < NT:
                nc.vector.tensor_copy(sums[1 - a][:, 0:step, :], sums[a][:, 0:step, :])
                link(nc.vector.tensor_tensor(sums[1 - a][:, step:, :], sums[a][:, step:, :], sums[a][:, :NT - step, :], ALU.add))
                a, step = 1 - a, 2 * step
            upto, rank = sums[a], sums[1 - a]
            link(nc.vector.tensor_scalar(blocks_i[:, :], upto[:, NT - 1, :], float(P - 1), None, ALU.add))
            link(nc.vector.tensor_scalar(blocks_i[:, :], blocks_i[:, :], int(math.log2(P)), None, ALU.arith_shift_right))
            link(nc.vector.tensor_copy(ends[0][:, :], blocks_i[:, :]))
            link(nc.vector.tensor_copy(starts[:, :], ends[0][:, :]))
            b, step = 0, 1
            while step < E:
                nc.vector.tensor_copy(ends[1 - b][:, 0:step], ends[b][:, 0:step])
                link(nc.vector.tensor_tensor(ends[1 - b][:, step:], ends[b][:, step:], ends[b][:, :E - step], ALU.add))
                b, step = 1 - b, 2 * step
            link(nc.vector.tensor_tensor(starts[:, :], ends[b][:, :], starts[:, :], ALU.subtract))
            link(nc.vector.tensor_scalar(starts[:, :], starts[:, :], float(P), None, ALU.mult))
            link(nc.vector.tensor_tensor(rank[:, :, :], upto[:, :, :], count_ps[:, 0, :].rearrange("p (t e) -> p t e", e=E), ALU.subtract))
            link(nc.vector.tensor_tensor(rank[:, :, :], rank[:, :, :], count_ps[:, 1, :].rearrange("p (t e) -> p t e", e=E), ALU.add))
            link(nc.vector.tensor_tensor(rank[:, :, :], rank[:, :, :], starts[:, :].unsqueeze(1).to_broadcast([P, NT, E]), ALU.add))
            for c in range(2):
                link(nc.vector.tensor_tensor(tmp[:, :, :], rank[:, :, :], chosen[:, c], ALU.mult))
                link(nc.vector.tensor_reduce(place_f[:, c], tmp[:, :, :], AX.X, ALU.add))
            nc.vector.tensor_copy(place[:, :, :], place_f[:, :, :]).then_inc(f_placed, 1)
            link(nc.vector.tensor_tensor(beyond[:, :, :], number.unsqueeze(2).to_broadcast([P, BLOCKS, E]),
                                         ends[b][:, :].unsqueeze(1).to_broadcast([P, BLOCKS, E]), ALU.is_ge))
            link(nc.vector.tensor_reduce(expert_f[:, :], beyond[:, :, :], AX.X, ALU.add))
            nc.vector.tensor_scalar(expert[:, :], expert_f[:, :], float(E - 1), None, ALU.min).then_inc(f_experts, 1)
            dve.wait_ge(f_exp, 1)
            link(nc.vector.tensor_scalar(share[:, 1], lead[:, :], 1.0, None, ALU.add))
            link(nc.vector.reciprocal(share[:, 0], share[:, 1]))
            link(nc.vector.tensor_tensor(share[:, 1], share[:, 0], lead[:, :], ALU.mult))
            dve.wait_ge(f_experts, 1)

            def copy_w1(k, e):
                wait(dve, f_gelu, k.plus(-1))
                nc.vector.tensor_copy(w1_e[k.p][:, :], w1_sb[:, bass.ds(e, 1), :].squeeze(1)).then_inc(f_w1, 1)

            def copy_w2(k, e):
                wait(dve, f_y, k.plus(-1))
                nc.vector.tensor_copy(w2_e[k.p][:, :], w2_sb[:, bass.ds(e, 1), :].squeeze(1)).then_inc(f_w2, 1)

            def turn(k):
                dve.wait_ge(f_xT, k.plus(1))
                wait(dve, f_up, k.plus(-1))
                nc.vector.tensor_copy(xgT[k.p][:, :], xT_ps[:, k.p, 0:P]).then_inc(f_xTs, 1)

            def finish(k):
                dve.wait_ge(f_down, k.plus(1))
                wait(dve, f_ys[k.q], k.landed(-1))
                nc.vector.tensor_tensor(y[k.q][:, :], y_ps[:, k.p, 0:D], w2_e[k.p][:, F:], ALU.add).then_inc(f_y, 1)

            for k in (Block(0), Block(1)):
                e = expert_of(dve, k)
                copy_w1(k, e)
                copy_w2(k, e)
                turn(k)

            def step(k, more):
                if more:
                    e = expert_of(dve, k.later(2))
                    turn(k.later(2))
                    copy_w1(k.later(2), e)
                finish(k)
                if more:
                    copy_w2(k.later(2), e)

            blocks(dve, step, 2)

            for n in range(2 * NT):
                t, c = divmod(n, 2)
                dve.wait_ge(f_yg[n % YB], 16 * (n // YB + 1))
                if c:
                    dve.wait_ge(f_sum, n)
                nc.vector.scalar_tensor_tensor(acc[:, t, :], yg[:, n % YB, :], share[:, c, t:t + 1], acc[:, t, :],
                                               ALU.mult, ALU.add).then_inc(f_sum, 1)

        @block.tensor
        def _(pe):
            pe.wait_ge(f_either, 1)
            pe.wait_ge(f_loaded, 4 * 16)
            flat = either[:, :, :].rearrange("p t e -> p (t e)")
            nc.tensor.matmul(count_ps[:, 0, :], ones, flat, start=True, stop=True)
            nc.tensor.matmul(count_ps[:, 1, :], above, flat, start=True, stop=True).then_inc(f_counted, 1)

            def turn_x(k):
                pe.wait_ge(f_xg[k.q], k.landed())
                wait(pe, f_xTs, k.plus(-1))
                nc.tensor.transpose(xT_ps[:, k.p, 0:P], xg[k.q][:, :], ident[:, :]).then_inc(f_xT, 1)

            def up(k):
                pe.wait_ge(f_w1, k.plus(1))
                pe.wait_ge(f_xTs, k.plus(1))
                wait(pe, f_gelu, k.plus(-1))
                for c in range(FC):
                    last = nc.tensor.matmul(h_ps[:, k.p, c * P:c * P + P], w1_e[k.p][:, c * P:c * P + P], xgT[k.p][:, :],
                                            start=True, stop=True)
                last.then_inc(f_up, 1)

            def down(k):
                pe.wait_ge(f_w2, k.plus(1))
                pe.wait_ge(f_gelu, k.plus(1))
                wait(pe, f_y, k.plus(-1))
                for c in range(FC):
                    last = nc.tensor.matmul(y_ps[:, k.p, 0:D], h[k.p][:, c, :], w2_e[k.p][:, c * D:c * D + D],
                                            start=c == 0, stop=c == FC - 1)
                last.then_inc(f_down, 1)

            turn_x(Block(0))
            turn_x(Block(1))
            up(Block(0))

            def step(k, more):
                if more:
                    turn_x(k.later(2))
                if k.turn is not None or k.n + 1 < BLOCKS:
                    up(k.later(1))
                down(k)

            blocks(pe, step, 2)


def kernel(**inputs):
    import numpy as _np
    import concourse.bacc as _bacc
    from concourse import mybir as _mybir
    from concourse.bass_utils import run_bass_kernel_spmd as _run

    w = _np.asarray(inputs["L0_attn_qkv_w"])
    bias = _np.asarray(inputs["L0_attn_qkv_b"])
    turned = _np.arange(D).reshape(H, 2, HALF)[:, ::-1].reshape(D)
    wq, wk, wv = w[0:D], w[D:2 * D], w[2 * D:3 * D]
    bq, bk, bv = bias[0:D], bias[D:2 * D], bias[2 * D:3 * D]
    named = {
        "x": inputs["L0_attn_x"],
        "wqkv": _np.concatenate([wq, wq[turned], wk, wk[turned], wv]).T,
        "qkb": _np.stack([bq, bq[turned], bk, bk[turned]], 1),
        "vb": bv,
        "wo": _np.asarray(inputs["L0_attn_out_w"]).T,
        "ob": inputs["L0_attn_out_b"],
        "rope": rope_tables(),
        "gw": inputs["L0_ffn_gate_w"],
        "w1": _np.concatenate([_np.asarray(inputs["L0_ffn_w1"]).transpose(1, 0, 2),
                               _np.asarray(inputs["L0_ffn_b1"]).reshape(E, FC, P).transpose(2, 0, 1)], 2),
        "w2": _np.asarray(inputs["L0_ffn_w2"]).reshape(E, FC, P, D).transpose(2, 0, 1, 3),
        "b2": inputs["L0_ffn_b2"],
        "route": routing_tables(),
    }
    nc = _bacc.Bacc("TRN2", target_bir_lowering=False, num_devices=1)
    arrays, args = {}, []
    for name, a in named.items():
        a = _np.ascontiguousarray(a)
        arrays[f"in_{name}_dram"] = a
        args.append(nc.dram_tensor(f"in_{name}_dram", a.shape, _mybir.dt.from_np(a.dtype), kind="ExternalInput").ap())
    args.append(nc.dram_tensor("out_0_dram", (NB, S, D), _mybir.dt.float32, kind="ExternalOutput").ap())
    block_kernel(nc, *args)
    r = _run(nc, [arrays], core_ids=[0])
    return r.results[0]["out_0_dram"]
```

```python
import math
from contextlib import ExitStack

import numpy as np

import concourse.bass as bass
from concourse import mybir

F32 = mybir.dt.float32
F32R = mybir.dt.float32r
U32, I32 = mybir.dt.uint32, mybir.dt.int32
BF16 = mybir.dt.bfloat16
ALU = mybir.AluOpType
ACT = mybir.ActivationFunctionType
AX = mybir.AxisListType

NB, S, D = 8, 512, 128
H, HD = 16, 8
HALF = HD // 2
P = 128
TJ = S // P
NT = NB * TJ
G = 4
NI = H // G
E, F = 8, 512
EPS = 1e-5
SCALE = 1.0 / math.sqrt(HD)
NEG = -1e38
SLOTS = 2
ST_BANKS = 3
UNITS = 12
CHUNKS = [[(0, 0, 512)], [(0, 1, 384)], [(0, 2, 256), (256, 3, 128)]]
CHUNK_AT, CHUNK_W = [0, 512, 896], [512, 384, 384]
PW = sum(CHUNK_W)
BLOCKS = (2 * NB * S + E * (P - 1)) // P + 1
TURN = 4
BLOCKS += -BLOCKS % TURN
assert BLOCKS % TURN == 0
FC = F // P
EXPERTS_AT = 4
SCATTERS = 5
GATHERS = 2 * NT // (NB - EXPERTS_AT) // NI
CLEAR = 6
PIECES = 5 * 16


def rope_tables():
    inv = (1.0 / 10000.0 ** (np.arange(HALF, dtype=np.float32) / np.float32(HALF))).astype(np.float32)
    angle = np.outer(np.arange(S, dtype=np.float32), inv).astype(np.float32)
    cos, sin = np.cos(angle).T, np.sin(angle).T
    cos8 = np.concatenate([cos, cos], 0)
    sin8 = np.concatenate([-sin, sin], 0)
    return np.tile(np.stack([cos8, sin8], 1), (H, 1, 1)).astype(np.float32)


def routing_tables():
    return np.concatenate([np.tile(np.arange(E, 0, -1), (P, 1)), np.tile(np.arange(BLOCKS), (P, 1)),
                           np.ones((P, P)), np.triu(np.ones((P, P)), 1)], 1).astype(np.float32)


class Batch:

    def __init__(self, n, turn=None):
        self.n, self.turn = n, turn

    def at(self, count, each):
        return count if self.turn is None else self.turn * int(2 * each) + count

    def plus(self, k):
        return Batch(self.n + k, self.turn)




PAIRS = 6


def slots_of(n):
    more, most = n + 1 < NB, n + 2 < NB
    extras = [("", False), ("", False), ("", False), ("OP", n > 0)]
    out = []
    for i in range(NI):
        pairs = [[("S", i, p)] if more else [] for p in range(PAIRS)]
        if not more and i == 0:
            pairs[1] = [("S", i, 1)]
        name, there = extras[i]
        out += pairs[0] + pairs[1] + pairs[2] + pairs[3] + ([name] if there else []) + pairs[4]
        out += pairs[5] + ([("N", i)] if i > 0 or n > 0 else []) + (["V"] if i == 3 and more else [])
    return out


def ring_of(n):
    out = []
    for i in range(NI):
        for pair in range(PAIRS):
            out += [("T", i, pair, h) for h in range(2)]
            if pair == 3 and i < 2 and n + 2 < NB:
                out += [("QK"[i], h) for h in range(2)]
            if pair == 4 and i == 2 and n > 0:
                out.append("AT")
    return out


RING_PRO = [("QK"[k], h, b) for b in range(2) for k in range(2) for h in range(2)]
RING_START = [len(RING_PRO)]
for _n in range(NB):
    RING_START.append(RING_START[-1] + len(ring_of(_n)))
RING_FULL = len(ring_of(1))


def ring(key, b=None, where=None):
    if where == "pro":
        return RING_PRO.index(key)
    if where == "epi":
        return RING_START[NB]
    return b.at(RING_START[b.n] + ring_of(b.n).index(key), RING_FULL)


PRO = [("XT", 0), ("XT", 1), ("V", 0)]
PRO += [("XT", b) for b in range(2, NB)] + ["GT"] + [("S", i, p) for i in range(NI) for p in range(PAIRS)] + ["CT"]
EPI = ["N", "OP"]
START = [len(PRO)]
for _n in range(NB):
    START.append(START[-1] + len(slots_of(_n)))
FULL = len(slots_of(1))
assert all(len(slots_of(n)) == FULL for n in range(1, NB - 2))


def slot(key, b=None, where=None):
    if where == "pro":
        s = PRO.index(key)
    elif where == "epi":
        s = START[NB] + EPI.index(key)
    else:
        s = START[b.n] + slots_of(b.n).index(key)
        return s % SLOTS, b.at(s // SLOTS + 1, FULL / SLOTS)
    return s % SLOTS, s // SLOTS + 1


def block_kernel(nc, x, wqkv, qkb, vb, wo, ob, rope, gw, w1, w2, b2, route, out):
    ctx = ExitStack()
    with ctx:
        def sb(name, shape, dt=F32):
            return ctx.enter_context(nc.sbuf_tensor(name, shape, dt))

        def sem(name):
            return ctx.enter_context(nc.semaphore(name))

        acc = sb("acc", [P, NT, D])
        xn_room = sb("xn_room", [P, E, F + FC])
        xn = xn_room[:, :, :].rearrange("p e f -> p (e f)")[:, 0:NT * D].rearrange("p (t d) -> p t d", d=D)
        logits = sb("logits", [P, NT, E])
        ident = sb("ident", [P, P])
        xnT = sb("xnT", [P, NB * S])
        stacks = [sb(f"stack{p}", [P, 2, NI, S], F32R) for p in range(2)]
        stack_q, stack_k = ([t[:, w] for t in stacks] for w in range(2))
        v32 = [sb(f"v32_{p}", [P, TJ, H, 32]) for p in range(2)]
        probs = [sb(f"probs{p}", [P, G, PW]) for p in range(2)]
        xTb = [sb(f"xTb{p}", [P, S]) for p in range(2)]
        scratch = sb("scratch", [P, 6 * S])
        ev = scratch[:, 0:4 * S].rearrange("p (m t) -> p m t", m=4)
        qk = scratch[:, 4 * S:].rearrange("p (k t) -> p k t", k=2)
        halves = sb("halves", [P, 4, S], F32R)
        high, low = (halves[:, 2], halves[:, 1]), (halves[:, 0], halves[:, 3])
        rope_sb = sb("rope_sb", [P, 2, S])
        w_sb = sb("w_sb", [P, 5 * D])
        wo_sb = sb("wo_sb", [P, D])
        gw_sb = sb("gw_sb", [P, E])
        qkb_sb = sb("qkb_sb", [P, 4])
        vb_sb = sb("vb_sb", [P, D])
        ob_sb = sb("ob_sb", [P, D])
        o_sb = [sb(f"o_sb{p}", [P, S]) for p in range(2)]
        attn = [sb(f"attn{p}", [P, TJ, D]) for p in range(2)]
        attnT = sb("attnT", [P, S])
        stats = sb("stats", [P, NT, 6])
        mv = sb("mv", [P, NT, 2])
        rstd = sb("rstd", [P, NT])
        half = sb("half", [P, TJ])
        part = [sb(f"part{p}", [P, G, 3]) for p in range(2)]
        nm = [sb(f"nm{p}", [P, G, TJ]) for p in range(2)]
        mrow = [sb(f"mrow{p}", [G * TJ, 2, P], F32R) for p in range(NI)]
        zeros = sb("zeros", [32, S], F32R)
        rec = sb("rec", [P, TJ, G])
        identb = sb("identb", [P, P], BF16)
        maskb = sb("maskb", [P, 2, P], BF16)

        w1_sb = xn_room
        w2_sb = probs[0][:, :, :].rearrange("p g w -> p (g w)").rearrange("p (e f) -> p e f", e=E)
        assert G * PW == E * (F + D)

        def parts(room, *shapes):
            views, at = [], 0
            for shape in shapes:
                n = math.prod(shape)
                v = room[:, at:at + n]
                views.append(v if len(shape) == 1 else v.rearrange("p (a b) -> p a b", a=shape[0]) if len(shape) == 2
                             else v.rearrange("p (a b c) -> p a b c", a=shape[0], b=shape[1]))
                at += n
            return views

        h, w1_e, xgT, y = parts(scratch, (2, FC, P), (2, F + FC), (2, P), (TURN, D))
        h, w1_e, xgT, y = ([v[:, k] for k in range(v.shape[1])] for v in (h, w1_e, xgT, y))
        w2_e = [sb(f"w2_e{p}", [P, F + D]) for p in range(2)]
        xg = [sb(f"xg{p}", [P, D]) for p in range(TURN)]
        YB = 4
        yg = sb("yg", [P, YB, D])
        share = sb("share", [P, 2, NT])
        place = sb("place", [P, 2, NT], U32)
        expert = sb("expert", [P, BLOCKS], I32)
        blocks_i = sb("blocks_i", [P, E], I32)
        chosen, lower, tmp, either, sums, beyond, blank, table, best, lead, ends, starts, expert_f, place_f = parts(
            probs[1][:, :, :].rearrange("p g w -> p (g w)"), (2, NT, E), (NT, E), (NT, E), (NT, E), (4, NT, E), (BLOCKS, E),
            (6, D), (E + BLOCKS + 2 * P,), (2, NT), (NT,), (2, E), (E,), (BLOCKS,), (2, NT))
        sums, ends = [sums[:, k] for k in range(4)], [ends[:, k] for k in range(2)]
        prefer, number = table[:, 0:E], table[:, E:E + BLOCKS]
        ones, above = table[:, E + BLOCKS:E + BLOCKS + P], table[:, E + BLOCKS + P:]

        st = ctx.enter_context(nc.psum_tensor("st", [P, ST_BANKS, 512], F32))
        wk = ctx.enter_context(nc.psum_tensor("wk", [P, SLOTS, 2, 512], F32))
        po = ctx.enter_context(nc.psum_tensor("po", [P, 512], F32))

        h_ps, y_ps, xT_ps = [st[:, k] for k in range(2)], [st[:, 2], po], [wk[:, k, 0] for k in range(2)]

        xg_dram = nc.dram_tensor("xg_dram", (BLOCKS * P, D), F32, kind="Internal").ap()
        y_dram = nc.dram_tensor("y_dram", (BLOCKS * P, D), F32, kind="Internal").ap()
        out_v = out.rearrange("b (j p) d -> p (b j) d", p=P)

        f_loaded = sem("f_loaded")
        f_blank = sem("f_blank")
        f_blanked = sem("f_blanked")
        f_route = sem("f_route")
        f_either = sem("f_either")
        f_counted = sem("f_counted")
        f_lead = sem("f_lead")
        f_exp = sem("f_exp")
        f_placed = sem("f_placed")
        f_experts = sem("f_experts")
        f_scattered = sem("f_scattered")
        f_xg = [sem(f"f_xg{p}") for p in range(TURN)]
        f_w1 = sem("f_w1")
        f_w2 = sem("f_w2")
        f_xT = sem("f_xT")
        f_xTs = sem("f_xTs")
        f_up = sem("f_up")
        f_gelu = sem("f_gelu")
        f_down = sem("f_down")
        f_y = sem("f_y")
        f_ys = [sem(f"f_ys{p}") for p in range(TURN)]
        f_yg = [sem(f"f_yg{k}") for k in range(YB)]
        f_sum = sem("f_sum")
        f_out = sem("f_out")
        f_route_in = sem("f_route_in")
        f_counts = sem("f_counts")
        f_shares = sem("f_shares")

        s_x = [sem(f"s_x{b}") for b in range(NB)]
        s_c = sem("s_c")
        s_ones = sem("s_ones")
        s_consts = sem("s_consts")
        s_stat = sem("s_stat")
        s_eps = sem("s_eps")
        s_rstd = sem("s_rstd")
        s_xn = sem("s_xn")
        s_chain = sem("s_chain")
        s_pc = sem("s_pc")
        s_xr = sem("s_xr")
        s_xnT = sem("s_xnT")
        xtb = [sem(f"xtb{p}") for p in range(2)]
        wk_full = [sem(f"wk_full{k}") for k in range(SLOTS)]
        wk_free = [sem(f"wk_free{k}") for k in range(SLOTS)]
        st_full = sem("st_full")
        st_free = sem("st_free")
        masked = sem("masked")
        pv_done = sem("pv_done")
        o_evac = sem("o_evac")
        v_ready = sem("v_ready")
        roped = sem("roped")
        split = sem("split")
        stacked = [sem(f"stacked{i}") for i in range(NI)]
        part_done = sem("part_done")
        nm_done = sem("nm_done")
        mrow_done = sem("mrow_done")
        mstored = sem("mstored")
        mrows = [sem(f"mrows{i}") for i in range(NI)]
        attn_done = sem("attn_done")
        acc_done = sem("acc_done")
        s_out = sem("s_out")
        s_zero = sem("s_zero")
        s_red = sem("s_red")
        s_rp = sem("s_rp")
        s_nt = sem("s_nt")
        s_op = sem("s_op")
        s_mt = sem("s_mt")
        s_vz = sem("s_vz")
        s_mv = sem("s_mv")
        s_hi = sem("s_hi")
        s_mh = sem("s_mh")
        s_rec = sem("s_rec")
        s_at = sem("s_at")

        x_v = x.rearrange("b (j p) d -> p b j d", p=P)
        out_v = out.rearrange("b (j p) d -> p (b j) d", p=P)
        m_dram = nc.dram_tensor("m_dram", (NI, 2, G * TJ, P), F32, kind="Internal").ap()
        N_CONST = 7 * 16

        def wait(eng, s, v):
            if not (isinstance(v, int) and v <= 0):
                eng.wait_ge(s, v)

        def qrow(t, i, r, n=HD):
            return t.rearrange("(g r) i t -> i r g t", g=G)[i, r:r + n]


        def loops(eng, step, experts):
            for n in range(NB):
                if n == EXPERTS_AT:
                    experts()
                step(Batch(n))

        class Block:
            def __init__(self, n, turn=None):
                self.n, self.turn, self.p, self.q = n, turn, n % 2, n % TURN

            def plus(self, v):
                return self.times(1, v)

            def times(self, v, c=0):
                return self.n * v + c if self.turn is None else self.turn * (TURN * v) + (self.n * v + c)

            def landed(self, c=0):
                v = 16 * (self.n // TURN + 1 + c)
                return v if self.turn is None else self.turn * 16 + v

            def later(self, v):
                return Block(self.n + v, self.turn)

        def blocks(eng, body, ahead):
            for n in range(TURN):
                body(Block(n), True)
            with eng.Fori(1, BLOCKS // TURN - 1) as turn:
                for n in range(TURN):
                    body(Block(n, turn), True)
            for n in range(BLOCKS - TURN, BLOCKS):
                body(Block(n), n + ahead < BLOCKS)

        def expert_of(eng, k):
            at = k.plus(0)
            return eng.value_load(expert[0:1, at:at + 1] if isinstance(at, int) else expert[0:1, bass.ds(at, 1)],
                                  min_val=0, max_val=E - 1)

        def experts_done(eng):
            eng.wait_ge(f_y, BLOCKS)
            for q in range(TURN):
                eng.wait_ge(f_ys[q], 16 * (BLOCKS // TURN))

        block = ctx.enter_context(nc.Block())

        @block.sync
        def _(sp):
            sp.dma_start(acc[:, 0:TJ, :], x_v[:, 0]).then_inc(s_x[0], 16)
            sp.dma_start(w_sb[:, :], wqkv).then_inc(s_c, 16)
            sp.dma_start(qkb_sb[:, :], qkb).then_inc(s_c, 16)
            sp.dma_start(rope_sb[:, :, :], rope).then_inc(s_c, 16)
            sp.dma_start(acc[:, TJ:2 * TJ, :], x_v[:, 1]).then_inc(s_x[1], 16)
            sp.dma_start(vb_sb[:, :], vb.partition_broadcast(P)).then_inc(s_c, 16)
            sp.dma_start(ob_sb[:, :], ob.partition_broadcast(P)).then_inc(s_c, 16)
            sp.dma_start(wo_sb[:, :], wo).then_inc(s_c, 16)
            sp.dma_start(gw_sb[:, :], gw).then_inc(s_c, 16)
            for b in range(2, NB):
                sp.dma_start(acc[:, TJ * b:TJ * b + TJ, :], x_v[:, b]).then_inc(s_x[b], 16)

            def load_xTb(b):
                p = b.n % 2
                wait(sp, s_xnT, b.at(b.n + 1, 1))
                wait(sp, v_ready, b.at(b.n - 1, 1))
                col = b.at(b.n * S, S)
                src = xnT[:, col:col + S] if isinstance(col, int) else xnT[:, bass.ds(col, S)]
                sp.dma_start(xTb[p][:, :], src).then_inc(xtb[p], 16)

            def stack(b, i):
                p = b.n % 2
                if b.n >= 2:
                    sp.wait_ge(st_full, ring(("T", i, PAIRS - 1, 1), b.plus(-2)) + 1)
                wait(sp, split, b.at(2 * b.n + 2, 2))
                wait(sp, stacked[i], b.at(PIECES * b.n, PIECES))
                src = slice(32 * i, 32 * i + 32)
                both = stacks[p][:, :, i, :]
                for dst, what in ((both[0:P:4, 0], halves[src, 2]), (both[0:P:4, 1], halves[src, 1]),
                                  (both[1:P:4], halves[src, 2:4]), (both[2:P:4], halves[src, 0:2]),
                                  (both[3:P:4, 0], zeros[:, :])):
                    sp.dma_start(dst.bitcast(F32), what.bitcast(F32)).then_inc(stacked[i], 16)

            def put_mrows(b, i):
                wait(sp, mrow_done, b.at(NI * b.n + i + 1, NI))
                sp.dma_start(m_dram[i].rearrange("r (g j) t -> (g j) r t", g=G),
                             mrow[i][:, :, :].bitcast(F32)).then_inc(mstored, 16)
                sp.wait_ge(mstored, b.at(16 * (NI * b.n + i + 1), 16 * NI))
                wait(sp, mrows[i], b.at(32 * b.n, 32))
                sp.wait_ge(stacked[i], b.at(PIECES * (b.n + 1), PIECES))
                for r in range(2):
                    sp.dma_start(stack_q[b.n % 2][3 + 4 * r:P:32, i, :].bitcast(F32),
                                 m_dram[i, r].rearrange("(g j) t -> g (j t)", g=G)).then_inc(mrows[i], 16)

            sp.dma_start(table[:, :], route).then_inc(f_route_in, 16)
            sp.wait_ge(s_zero, 1)
            sp.wait_ge(s_ones, 2)
            load_xTb(Batch(0))
            load_xTb(Batch(1))
            for i in range(NI):
                stack(Batch(0), i)
            for i in range(NI):
                stack(Batch(1), i)
            load_xTb(Batch(2))
            sp.wait_ge(f_blank, 1)
            for k in range(0, BLOCKS, CLEAR):
                sp.dma_start(xg_dram[k * P:(k + CLEAR) * P, :].rearrange("(k p) d -> p k d", p=P),
                             blank[:, :, :]).then_inc(f_blanked, 16)
            for i in range(NI - 1):
                put_mrows(Batch(0), i)

            def step(b):
                for i in range(NI):
                    if i == 0:
                        put_mrows(b, NI - 1)
                    elif b.n + 1 < NB:
                        put_mrows(b.plus(1), i - 1)
                    if b.n + 2 < NB:
                        stack(b.plus(2), i)
                if b.n + 3 < NB:
                    load_xTb(b.plus(3))

            def experts():
                sp.wait_ge(f_scattered, 16 * 2 * NT)
                for n in range(TURN):
                    load(Block(n))
                blocks(sp, step_x, TURN)
                store(Block(BLOCKS - 2))
                store(Block(BLOCKS - 1))

            def load(k):
                wait(sp, f_xT, k.plus(1 - TURN))
                at = k.times(P)
                src = xg_dram[at:at + P, :] if isinstance(at, int) else xg_dram[bass.ds(at, P), :]
                sp.dma_start(xg[k.q][:, :], src).then_inc(f_xg[k.q], 16)

            def store(k):
                sp.wait_ge(f_y, k.plus(1))
                at = k.times(P)
                dst = y_dram[at:at + P, :] if isinstance(at, int) else y_dram[bass.ds(at, P), :]
                sp.dma_start(dst, y[k.q][:, :]).then_inc(f_ys[k.q], 16)

            def step_x(k, more):
                if more:
                    load(k.later(TURN))
                if k.turn is not None or k.n >= 2:
                    store(k.later(-2))

            loops(sp, step, experts)
            sp.wait_ge(f_sum, 2 * NT)
            sp.wait_ge(acc_done, NB - 1)
            last = TJ * (NB - 1)
            sp.dma_start(out_v[:, 0:last, :], acc[:, 0:last, :]).then_inc(f_out, 16)
            sp.wait_ge(acc_done, NB)
            sp.dma_start(out_v[:, last:, :], acc[:, last:, :]).then_inc(f_out, 16)
            sp.wait_ge(f_out, 32)

        @block.gpsimd
        def _(pool):
            for t in stack_k:
                nc.gpsimd.memset(t.bitcast(F32), 1.0).then_inc(s_ones, 1)
            nc.gpsimd.memset(zeros[:, :].bitcast(F32), 0.0).then_inc(s_zero, 1)
            nc.gpsimd.memset(ident[:, :], 0.0).then_inc(s_pc, 1)
            nc.gpsimd.memset(maskb[:, :, :], 0.0).then_inc(s_pc, 1)
            nc.gpsimd.memset(half[:, :], -0.5).then_inc(s_pc, 1)
            nc.gpsimd.memset(blank[:, :, :], 0.0).then_inc(f_blank, 1)
            pool.wait_ge(s_pc, 3)
            nc.gpsimd.affine_select(out=ident[:, :], in_=ident[:, :], pattern=[[-1, P]], compare_op=ALU.not_equal,
                                    fill=1.0, base=0, channel_multiplier=1).then_inc(s_pc, 1)
            nc.gpsimd.affine_select(out=maskb[:, :, :], in_=maskb[:, :, :], pattern=[[0, 2], [-1, P]],
                                    compare_op=ALU.is_ge, fill=NEG, base=0, channel_multiplier=1).then_inc(s_pc, 1)
            pool.wait_ge(s_pc, 5)
            nc.gpsimd.tensor_copy(identb[:, :], ident[:, :]).then_inc(s_consts, 1)
            for b in range(NB):
                pool.wait_ge(s_eps, b + 1)
                nc.gpsimd.tensor_tensor(rstd[:, TJ * b:TJ * b + TJ], rstd[:, TJ * b:TJ * b + TJ], half[:, :],
                                        ALU.pow).then_inc(s_rstd, 1)
            pool.wait_ge(s_c, N_CONST)

            def rope_qk(b, k):
                key = ("QK"[k], 1)
                pool.wait_ge(st_free, (ring(key, b.plus(-2)) if b.n > 1 else ring((*key, b.n), None, "pro")) + 1)
                wait(pool, split, b.at(2 * b.n, 2))
                a_, b_ = ev[:, 2 * k], ev[:, 2 * k + 1]
                nc.gpsimd.tensor_tensor(a_, a_, rope_sb[:, 0], ALU.mult).then_inc(s_rp, 1)
                nc.gpsimd.tensor_tensor(b_, b_, rope_sb[:, 1], ALU.mult).then_inc(s_rp, 1)
                pool.wait_ge(s_rp, b.at(4 * b.n + 2 * k + 2, 4))
                nc.gpsimd.tensor_tensor(qk[:, k], a_, b_, ALU.add).then_inc(roped, 1)

            for b in range(2):
                rope_qk(Batch(b), 0)
                rope_qk(Batch(b), 1)
            for b in range(NB):
                pool.wait_ge(s_xn, TJ * (b + 1))
                t = acc[:, TJ * b:TJ * b + TJ, :]
                nc.gpsimd.tensor_tensor(t, t, ob_sb[:, :].unsqueeze(1).to_broadcast([P, TJ, D]), ALU.add).then_inc(s_xr, 1)

            def scatter(n):
                t, c = divmod(n, 2)
                nc.gpsimd.indirect_dma_start(xg_dram[:, :], bass.IndirectOffsetOnAxis(place[:, c, t:t + 1], 0),
                                             xn[:, t, :], None).then_inc(f_scattered, 16)

            def gather(n):
                t, c = divmod(n, 2)
                wait(pool, f_sum, n - YB + 1)
                nc.gpsimd.indirect_dma_start(yg[:, n % YB, :], None, y_dram[:, :],
                                             bass.IndirectOffsetOnAxis(place[:, c, t:t + 1], 0)).then_inc(f_yg[n % YB], 16)

            def step(b):
                for i in range(NI):
                    gpar = i % 2
                    period = NI * b.n + i
                    for u in range(PAIRS):
                        c, gp = u % 3, u // 3
                        pool.wait_ge(st_free, ring(("T", i, u, 1), b) + 1)
                        at = CHUNK_AT[c]
                        if c < 2:
                            v = probs[gpar][:, 2 * gp:2 * gp + 2, at:at + P]
                            pat = [[0, 2], [1, P]]
                            nc.gpsimd.affine_select(out=v, in_=v, pattern=pat, compare_op=ALU.is_ge, fill=0.0,
                                                    base=0, channel_multiplier=-1).then_inc(masked, 1)
                        else:
                            for k in range(2):
                                v = probs[gpar][:, 2 * gp:2 * gp + 2, at + 256 * k:at + 256 * k + P]
                                last = nc.gpsimd.affine_select(out=v, in_=v, pattern=[[0, 2], [1, P]],
                                                               compare_op=ALU.is_ge, fill=0.0, base=0,
                                                               channel_multiplier=-1)
                                last.then_inc(masked, 1)
                    if i < 2 and b.n + 2 < NB:
                        rope_qk(b.plus(2), i)
                    if b.n < EXPERTS_AT:
                        if period == 0:
                            pool.wait_ge(f_placed, 1)
                            pool.wait_ge(f_blanked, 16 * (BLOCKS // CLEAR))
                        for n in range(SCATTERS * period, min(SCATTERS * (period + 1), 2 * NT)):
                            scatter(n)
                    else:
                        for n in range(GATHERS):
                            gather(GATHERS * (period - NI * EXPERTS_AT) + n)

            loops(pool, step, lambda: experts_done(pool))

        @block.scalar
        def _(act):
            def evac_qk(b, k, where=None):
                wait(act, roped, b.at(2 * (b.n - 1) + k + 1, 2))
                for h in range(2):
                    n = ring(("QK"[k], h, b.n), None, where) if where else ring(("QK"[k], h), b.plus(-2))
                    m = 2 * k + h
                    act.wait_ge(st_full, n + 1)
                    nc.scalar.activation(ev[:, m], st[:, n % ST_BANKS, :], ACT.Identity, bias=qkb_sb[:, m:m + 1]).then_inc(st_free, 1)

            def evac_plain(key, b, where, dst, done, count):
                w, n = slot(key, b, where)
                act.wait_ge(wk_full[w], n)
                nc.scalar.activation(dst, wk[:, w, 0, :], ACT.Copy).then_inc(done, 1)
                act.wait_ge(done, count)
                act.sem_inc(wk_free[w], 1)

            act.wait_ge(s_c, N_CONST)
            for b in range(2):
                evac_plain(("XT", b), None, "pro", xnT[:, S * b:S * b + S], s_xnT, b + 1)
            for b in range(2):
                evac_qk(Batch(b), 0, "pro")
                evac_qk(Batch(b), 1, "pro")
            for b in range(2, NB):
                evac_plain(("XT", b), None, "pro", xnT[:, S * b:S * b + S], s_xnT, b + 1)

            def evac_o(b, i):
                act.wait_ge(pv_done, b.at(NI * b.n + i + 1, NI))
                wait(act, s_nt, b.at(NI * b.n + i - 1, NI))
                nc.scalar.activation(o_sb[i % 2][:, :], po[:, :], ACT.Copy).then_inc(o_evac, 1)

            def evac_at(b, key_b, where):
                wait(act, s_op, b.at(b.n, 1))
                n = ring("AT", key_b, where)
                act.wait_ge(st_full, n + 1)
                nc.scalar.activation(attnT[:, :], st[:, n % ST_BANKS, :], ACT.Copy).then_inc(st_free, 1)

            def exps(b, i, pair):
                gp, c = divmod(pair, 3)
                group = NI * b.n + i
                if pair == 0:
                    wait(act, pv_done, b.at(group - 1, NI))
                if pair == 0 and group == 1:
                    act.wait_ge(f_shares, 1)
                    act.wait_ge(f_blanked, 16 * (BLOCKS // CLEAR))
                at, w = CHUNK_AT[c], CHUNK_W[c]
                for h in range(2):
                    n = ring(("T", i, pair, h), b)
                    act.wait_ge(st_full, n + 1)
                    nc.scalar.activation(probs[i % 2][:, 2 * gp + h, at:at + w], st[:, n % ST_BANKS, 0:w],
                                         ACT.Exp, scale=SCALE).then_inc(st_free, 1)

            def step(b):
                most = b.n + 2 < NB
                for i in range(NI):
                    if b.n == EXPERTS_AT - 1 and i == 2:
                        act.wait_ge(f_scattered, 16 * 2 * NT)
                        nc.scalar.dma_start(w1_sb[:, :, :], w1).then_inc(f_loaded, 16)
                    exps(b, i, 0)
                    exps(b, i, 1)
                    exps(b, i, 2)
                    exps(b, i, 3)
                    if i > 0 or b.n > 0:
                        evac_o(b if i else b.plus(-1), (i - 1) % NI)
                    if b.n == EXPERTS_AT - 1 and i == 3:
                        nc.scalar.dma_start(w2_sb[:, :, 0:F], w2).then_inc(f_loaded, 16)
                        nc.scalar.dma_start(w2_sb[:, :, F:], b2.partition_broadcast(P)).then_inc(f_loaded, 16)
                    if i < 2 and most:
                        evac_qk(b.plus(2), i)
                    exps(b, i, 4)
                    if i == 2 and b.n > 0:
                        evac_at(b.plus(-1), b, None)
                    exps(b, i, 5)

            def turn(k):
                act.wait_ge(f_xT, k.plus(1))
                wait(act, f_up, k.plus(-1))
                nc.scalar.activation(xgT[k.p][:, :], xT_ps[k.p][:, 0:P], ACT.Copy).then_inc(f_xTs, 1)

            def gelu(k):
                act.wait_ge(f_up, k.plus(1))
                act.wait_ge(f_w1, k.plus(1))
                wait(act, f_down, k.plus(-1))
                for c in range(FC):
                    last = nc.scalar.activation(h[k.p][:, c, :], h_ps[k.p][:, c * P:c * P + P], ACT.Gelu,
                                                bias=w1_e[k.p][:, F + c:F + c + 1])
                last.then_inc(f_gelu, 1)

            def step_x(k, more):
                if more:
                    turn(k.later(2))
                if k.turn is not None or k.n + 1 < BLOCKS:
                    gelu(k.later(1))

            def experts():
                act.wait_ge(split, 2 * (EXPERTS_AT + 2))
                turn(Block(0))
                turn(Block(1))
                gelu(Block(0))
                blocks(act, step_x, 2)
                experts_done(act)

            act.wait_ge(f_lead, 1)
            nc.scalar.activation(lead[:, :], lead[:, :], ACT.Exp).then_inc(f_exp, 1)
            loops(act, step, experts)
            evac_o(Batch(NB - 1), NI - 1)
            evac_at(Batch(NB - 1), None, "epi")


        @block.vector
        def _(dve):
            chain = [0]

            def link(ins):
                chain[0] += 1
                ins.then_inc(s_chain, 1)
                dve.wait_ge(s_chain, chain[0])

            for t in v32:
                nc.vector.memset(t[:, :, :, :], 0.0).then_inc(s_vz, 1)
            dve.wait_ge(s_vz, 2)
            for t in v32:
                nc.vector.memset(t[:, :, :, HD:HD + 1], 1.0).then_inc(s_vz, 1)
            for b in range(NB):
                dve.wait_ge(s_x[b], 16)
                for j in range(TJ):
                    t = TJ * b + j
                    nc.vector.bn_stats(stats[:, t, :], acc[:, t, :]).then_inc(s_stat, 1)
                dve.wait_ge(s_stat, TJ * (b + 1))
                for j in range(TJ):
                    t = TJ * b + j
                    nc.vector.bn_aggr(mv[:, t, :], stats[:, t, :]).then_inc(s_mv, 1)
                dve.wait_ge(s_mv, TJ * (b + 1))
                nc.vector.tensor_scalar_add(rstd[:, TJ * b:TJ * b + TJ], mv[:, TJ * b:TJ * b + TJ, 1],
                                            EPS).then_inc(s_eps, 1)
                dve.wait_ge(s_rstd, b + 1)
                for j in range(TJ):
                    t = TJ * b + j
                    nc.vector.tensor_scalar(xn[:, t, :], acc[:, t, :], mv[:, t, 0:1], rstd[:, t:t + 1],
                                            ALU.subtract, ALU.mult).then_inc(s_xn, 1)
                if b == 1:
                    pass

            def split_qk(b, k):
                dve.wait_ge(roped, b.at(2 * b.n + k + 1, 2))
                for p in range(NI):
                    wait(dve, stacked[p], b.at(PIECES * b.n, PIECES))
                nc.vector.tensor_copy(high[k], qk[:, k]).then_inc(s_hi, 1)
                dve.wait_ge(s_hi, b.at(2 * b.n + k + 1, 2))
                nc.vector.tensor_tensor(low[k], qk[:, k], high[k].bitcast(F32), ALU.subtract).then_inc(split, 1)

            def put_v(b, key, key_b, where):
                bank, n = slot(key, key_b, where)
                dve.wait_ge(wk_full[bank], n)
                wait(dve, pv_done, b.at(NI * (b.n - 1), NI))
                src = wk[:, bank, 0, :].rearrange("p (j h d) -> p j h d", j=TJ, h=H)
                bias = vb_sb[:, :].rearrange("p (h d) -> p h d", h=H).unsqueeze(1).to_broadcast([P, TJ, H, HD])
                nc.vector.tensor_tensor(v32[b.n % 2][:, :, :, 0:HD], src, bias, ALU.add).then_inc(v_ready, 1)
                dve.wait_ge(v_ready, b.at(b.n + 1, 1))
                dve.sem_inc(wk_free[bank], 1)

            def maxima(b, key_b, i, pair, where=None, turns=False):
                gp, c = divmod(pair, 3)
                if pair == 0:
                    wait(dve, s_mt, b.at(NI * b.n + i - 1, NI))
                w, n = slot(("S", i, pair), key_b, where)
                dve.wait_ge(wk_full[w], n)
                g = slice(2 * gp, 2 * gp + 2)
                if c == 0:
                    dst, src = part[i % 2][:, g, :], wk[:, w, :, 0:3 * P].rearrange("p h (u k) -> p h u k", u=3)
                else:
                    dst, src = nm[i % 2][:, g, c + 1], wk[:, w, :, 0:(c + 2) * P]
                if turns:
                    nc.vector.tensor_reduce(dst, src, AX.X, ALU.max, negate=True).then_inc(s_red, 1)
                else:
                    nc.vector.tensor_reduce(dst, src, AX.X, ALU.max, negate=True).then_inc(wk_free[w], 1)
                if pair == 5:
                    dve.wait_ge(wk_free[w], n)
                    nc.vector.tensor_copy(nm[i % 2][:, :, 0], part[i % 2][:, :, 0]).then_inc(nm_done, 1)
                    nc.vector.tensor_tensor(nm[i % 2][:, :, 1], part[i % 2][:, :, 1], part[i % 2][:, :, 2],
                                            ALU.min).then_inc(nm_done, 1)

            def max_rows(b, key, key_b, i, where):
                w, n = slot(key, key_b, where)
                dve.wait_ge(wk_full[w], n)
                wait(dve, mrows[i], b.at(32 * b.n, 32))
                src = wk[0:G * TJ, w, 0, 3 * P:4 * P]
                nc.vector.tensor_copy(mrow[i][:, 0, :], src).then_inc(s_mh, 1)
                dve.wait_ge(s_mh, b.at(NI * b.n + i + 1, NI))
                nc.vector.tensor_tensor(mrow[i][:, 1, :], src, mrow[i][:, 0, :].bitcast(F32),
                                        ALU.subtract).then_inc(mrow_done, 1)
                dve.wait_ge(mrow_done, b.at(NI * b.n + i + 1, NI))
                dve.sem_inc(wk_free[w], 1)

            def norm(b, key, key_b, i, where=None):
                bank, n = slot(key, key_b, where)
                dve.wait_ge(wk_full[bank], n)
                src = wk[:, bank, 0, :].rearrange("p (j g c) -> p j g c", j=TJ, g=G)
                nc.vector.reciprocal(rec[:, :, :], src[:, :, :, HD]).then_inc(s_rec, 1)
                dve.wait_ge(s_rec, b.at(NI * b.n + i + 1, NI))
                if i == 0:
                    wait(dve, s_at, b.at(b.n - 1, 1))
                dst = attn[b.n % 2][:, :, 32 * i:32 * i + 32].rearrange("p j (g d) -> p j g d", g=G)
                nc.vector.tensor_tensor(dst, src[:, :, :, 0:HD], rec[:, :, :].unsqueeze(3).to_broadcast([P, TJ, G, HD]),
                                        ALU.mult).then_inc(attn_done, 1)
                dve.wait_ge(attn_done, b.at(NI * b.n + i + 1, NI))
                dve.sem_inc(wk_free[bank], 1)

            def add_out(b, key_b, where=None):
                bank, n = slot("OP", key_b, where)
                dve.wait_ge(wk_full[bank], n)
                wait(dve, f_sum, GATHERS * (NI * (b.n + 1 - EXPERTS_AT) + 2) if key_b else 2 * NT)
                row = b.at(TJ * b.n, TJ)
                t = acc[:, row:row + TJ, :] if isinstance(row, int) else acc[:, bass.ds(row, TJ), :]
                nc.vector.tensor_tensor(t, wk[:, bank, 0, :].rearrange("p (j d) -> p j d", j=TJ), t,
                                        ALU.add).then_inc(acc_done, 1)
                dve.wait_ge(acc_done, b.at(b.n + 1, 1))
                dve.sem_inc(wk_free[bank], 1)

            b0, b1 = Batch(0), Batch(1)
            split_qk(b0, 0)
            split_qk(b0, 1)
            put_v(b0, ("V", 0), None, "pro")
            split_qk(b1, 0)
            split_qk(b1, 1)
            bank, n = slot("GT", None, "pro")
            dve.wait_ge(wk_full[bank], n)
            nc.vector.tensor_copy(logits[:, :, :], wk[:, bank, 0, 0:NT * E].rearrange("p (t e) -> p t e", e=E)).then_inc(wk_free[bank], 1)
            dve.wait_ge(wk_free[bank], n)
            dve.wait_ge(s_xr, NB)
            links = [0]

            def link(ins):
                links[0] += 1
                ins.then_inc(f_route, 1)
                dve.wait_ge(f_route, links[0])

            def along_e(v):
                return v.unsqueeze(2).to_broadcast([P, NT, E])

            prefers = prefer.unsqueeze(1).to_broadcast([P, NT, E])
            dve.wait_ge(f_route_in, 16)
            scores = logits
            for c in range(2):
                link(nc.vector.tensor_reduce(best[:, c], scores[:, :, :], AX.X, ALU.max))
                link(nc.vector.tensor_tensor(tmp[:, :, :], scores[:, :, :], along_e(best[:, c]), ALU.is_equal))
                link(nc.vector.tensor_tensor(tmp[:, :, :], tmp[:, :, :], prefers, ALU.mult))
                link(nc.vector.tensor_reduce(share[:, c], tmp[:, :, :], AX.X, ALU.max))
                link(nc.vector.tensor_tensor(chosen[:, c], prefers, along_e(share[:, c]), ALU.is_equal))
                if c == 0:
                    link(nc.vector.scalar_tensor_tensor(lower[:, :, :], chosen[:, 0], -3e38, logits[:, :, :],
                                                        ALU.mult, ALU.add))
                    scores = lower
            nc.vector.tensor_tensor(either[:, :, :], chosen[:, 0], chosen[:, 1], ALU.add).then_inc(f_either, 1)
            nc.vector.tensor_tensor(lead[:, :], best[:, 1], best[:, 0], ALU.subtract).then_inc(f_lead, 1)
            for i in range(NI):
                for pair in range(PAIRS):
                    turns = pair == 1 and i > 0
                    maxima(b0, None, i, pair, "pro", turns)
                    if turns:
                        dve.wait_ge(s_red, i)
                        max_rows(b0, ("S", i, 1), None, i - 1, "pro")

            bank, n = slot("CT", None, "pro")
            dve.wait_ge(wk_full[bank], n)
            for k in range(2):
                nc.vector.tensor_copy(sums[2 + k][:, :, :], wk[:, bank, 0, k * NT * E:(k + 1) * NT * E].rearrange(
                    "p (t e) -> p t e", e=E)).then_inc(f_counts, 1)
            dve.wait_ge(f_counts, 2)
            dve.sem_inc(wk_free[bank], 1)
            link(nc.vector.tensor_copy(sums[0][:, :, :], sums[2][:, :, :]))
            a, step = 0, 1
            while step < NT:
                nc.vector.tensor_copy(sums[1 - a][:, 0:step, :], sums[a][:, 0:step, :])
                link(nc.vector.tensor_tensor(sums[1 - a][:, step:, :], sums[a][:, step:, :], sums[a][:, :NT - step, :], ALU.add))
                a, step = 1 - a, 2 * step
            upto, rank = sums[a], sums[1 - a]
            link(nc.vector.tensor_scalar(blocks_i[:, :], upto[:, NT - 1, :], float(P - 1), None, ALU.add))
            link(nc.vector.tensor_scalar(blocks_i[:, :], blocks_i[:, :], int(math.log2(P)), None, ALU.arith_shift_right))
            link(nc.vector.tensor_copy(ends[0][:, :], blocks_i[:, :]))
            link(nc.vector.tensor_copy(starts[:, :], ends[0][:, :]))
            b, step = 0, 1
            while step < E:
                nc.vector.tensor_copy(ends[1 - b][:, 0:step], ends[b][:, 0:step])
                link(nc.vector.tensor_tensor(ends[1 - b][:, step:], ends[b][:, step:], ends[b][:, :E - step], ALU.add))
                b, step = 1 - b, 2 * step
            link(nc.vector.tensor_tensor(starts[:, :], ends[b][:, :], starts[:, :], ALU.subtract))
            link(nc.vector.tensor_scalar(starts[:, :], starts[:, :], float(P), None, ALU.mult))
            link(nc.vector.tensor_tensor(rank[:, :, :], upto[:, :, :], sums[2][:, :, :], ALU.subtract))
            link(nc.vector.tensor_tensor(rank[:, :, :], rank[:, :, :], sums[3][:, :, :], ALU.add))
            link(nc.vector.tensor_tensor(rank[:, :, :], rank[:, :, :], starts[:, :].unsqueeze(1).to_broadcast([P, NT, E]), ALU.add))
            for c in range(2):
                link(nc.vector.tensor_tensor(tmp[:, :, :], rank[:, :, :], chosen[:, c], ALU.mult))
                link(nc.vector.tensor_reduce(place_f[:, c], tmp[:, :, :], AX.X, ALU.add))
            nc.vector.tensor_copy(place[:, :, :], place_f[:, :, :]).then_inc(f_placed, 1)
            link(nc.vector.tensor_tensor(beyond[:, :, :], number.unsqueeze(2).to_broadcast([P, BLOCKS, E]),
                                         ends[b][:, :].unsqueeze(1).to_broadcast([P, BLOCKS, E]), ALU.is_ge))
            link(nc.vector.tensor_reduce(expert_f[:, :], beyond[:, :, :], AX.X, ALU.add))
            nc.vector.tensor_scalar(expert[:, :], expert_f[:, :], float(E - 1), None, ALU.min).then_inc(f_experts, 1)
            dve.wait_ge(f_exp, 1)
            link(nc.vector.tensor_scalar(share[:, 1], lead[:, :], 1.0, None, ALU.add))
            link(nc.vector.reciprocal(share[:, 0], share[:, 1]))
            nc.vector.tensor_tensor(share[:, 1], share[:, 0], lead[:, :], ALU.mult).then_inc(f_shares, 1)
            dve.wait_ge(f_experts, 1)


            def copy_w1(k, e):
                wait(dve, f_gelu, k.plus(-1))
                nc.vector.tensor_copy(w1_e[k.p][:, :], w1_sb[:, bass.ds(e, 1), :].squeeze(1)).then_inc(f_w1, 1)

            def copy_w2(k, e):
                wait(dve, f_y, k.plus(-1))
                nc.vector.tensor_copy(w2_e[k.p][:, :], w2_sb[:, bass.ds(e, 1), :].squeeze(1)).then_inc(f_w2, 1)

            def finish(k):
                dve.wait_ge(f_down, k.plus(1))
                wait(dve, f_ys[k.q], k.landed(-1))
                nc.vector.tensor_tensor(y[k.q][:, :], y_ps[k.p][:, 0:D], w2_e[k.p][:, F:], ALU.add).then_inc(f_y, 1)

            def step_x(k, more):
                if more:
                    e = expert_of(dve, k.later(2))
                    copy_w1(k.later(2), e)
                finish(k)
                if more:
                    copy_w2(k.later(2), e)


            def experts():
                dve.wait_ge(split, 2 * (EXPERTS_AT + 2))
                dve.wait_ge(f_loaded, 3 * 16)
                for k in (Block(0), Block(1)):
                    e = expert_of(dve, k)
                    copy_w1(k, e)
                    copy_w2(k, e)

                blocks(dve, step_x, 2)
                experts_done(dve)

            def add_expert(n):
                t, c = divmod(n, 2)
                dve.wait_ge(f_yg[n % YB], 16 * (n // YB + 1))
                wait(dve, f_sum, n)
                nc.vector.scalar_tensor_tensor(acc[:, t, :], yg[:, n % YB, :], share[:, c, t:t + 1], acc[:, t, :],
                                               ALU.mult, ALU.add).then_inc(f_sum, 1)

            def step(b):
                more, most = b.n + 1 < NB, b.n + 2 < NB
                for i in range(NI):
                    for pair in range(PAIRS):
                        if more:
                            maxima(b.plus(1), b, i, pair, None, pair == 1)
                        if pair == 1 and more:
                            dve.wait_ge(s_red, b.at(NI * b.n + i + NI, NI))
                        if pair == 1 and (more or i == 0):
                            max_rows(b if i == 0 else b.plus(1), ("S", i, 1), b, (i - 1) % NI, None)
                        if pair == 2 and i in (1, 2) and most:
                            split_qk(b.plus(2), i - 1)
                        if pair == 3 and i == 3 and b.n > 0:
                            add_out(b.plus(-1), b)
                        if pair == 5 and (i > 0 or b.n > 0):
                            norm(b if i else b.plus(-1), ("N", i), b, (i - 1) % NI)
                    if i == 3 and more:
                        put_v(b.plus(1), "V", b, None)
                    period = NI * (b.n - EXPERTS_AT) + i - 1
                    if period >= 0:
                        for n in range(GATHERS * period, GATHERS * (period + 1)):
                            add_expert(n)

            loops(dve, step, experts)
            for n in range(2 * NT - GATHERS, 2 * NT):
                add_expert(n)
            norm(Batch(NB - 1), "N", None, NI - 1, "epi")
            add_out(Batch(NB - 1), None, "epi")


        @block.tensor
        def _(pe):
            def fill(key, b, where=None):
                bank, n = slot(key, b, where)
                wait(pe, wk_free[bank], n - 1)
                return bank

            def scores(b, key_b, i, pair, where=None, turns=None):
                gp, c = divmod(pair, 3)
                q, k = stack_q[b.n % 2], stack_k[b.n % 2]
                w = fill(("S", i, pair), key_b, where)
                if turns is not None:
                    of, ti = turns
                    pe.wait_ge(nm_done, of.at(2 * (NI * of.n + ti + 1), 2 * NI))
                    nc.tensor.matmul(wk[0:G * TJ, w, 0, 3 * P:4 * P], nm[ti % 2][:, :, :].rearrange("p g j -> p (g j)"),
                                     ident[:, :], start=True, stop=True, skip_group_check=True).then_inc(s_mt, 1)
                if b.n >= NB:
                    pe.wait_ge(s_mt, of.at(NI * of.n + ti + 1, NI))
                    pe.sem_inc(wk_full[w], 1)
                    return
                for at, j in ([(0, 0), (P, 1)] if c == 0 else [(0, c + 1)]):
                    for h in range(2):
                        g = 2 * gp + h
                        r, width = slice(32 * g, 32 * g + 32), (j + 1) * P
                        nc.tensor.matmul(wk[:, w, h, at:at + width], q[r, i, j * P:j * P + P], k[r, i, 0:width],
                                         start=at == 0, stop=False, skip_group_check=True)
                for h in range(2):
                    if c == 0:
                        diag, mask = wk[:, w, h, :].rearrange("p (a t) -> p a t", a=2)[:, :, 0:P], maskb[:, :, :]
                    else:
                        diag, mask = wk[:, w, h, (c + 1) * P:(c + 2) * P], maskb[:, 0, :]
                    last = nc.tensor.matmul(diag, identb[:, :], mask, start=False, stop=True, skip_group_check=True)
                last.then_inc(wk_full[w], 1)

            def scores_t(b, i, pair):
                gp, c = divmod(pair, 3)
                n = ring(("T", i, pair, 0), b)
                if pair == 0:
                    pe.wait_ge(mrows[i], b.at(32 * (b.n + 1), 32))
                pe.wait_ge(st_free, n + 2 - ST_BANKS)
                q, k = stack_q[b.n % 2], stack_k[b.n % 2]
                for at, kt, w in CHUNKS[c]:
                    for h in range(2):
                        g = 2 * gp + h
                        r = slice(32 * g, 32 * g + 32)
                        last = nc.tensor.matmul(st[:, (n + h) % ST_BANKS, at:at + w], k[r, i, kt * P:kt * P + P],
                                                q[r, i, kt * P:S], start=True, stop=True, skip_group_check=True)
                        if at + w == CHUNK_W[c]:
                            last.then_inc(st_full, 1)

            def weigh(b, i, tiles):
                pe.wait_ge(masked, b.at(8 * (NI * b.n + i) + (5 if tiles[-1] == 0 else 6 if tiles[-1] == 1 else 8), 8 * NI))
                if 0 in tiles:
                    if i == 0:
                        pe.wait_ge(v_ready, b.at(b.n + 1, 1))
                    wait(pe, o_evac, b.at(NI * b.n + i, NI))
                for c in range(3):
                    for at, kt, w in CHUNKS[c]:
                        if kt in tiles:
                            for g in range(G):
                                o = CHUNK_AT[c] + at
                                last = nc.tensor.matmul(po[32 * g:32 * g + 32, kt * P:S], v32[b.n % 2][:, kt, 4 * i + g, :],
                                                        probs[i % 2][:, g, o:o + w], start=kt == 0, stop=kt == TJ - 1,
                                                        skip_group_check=True)
                if TJ - 1 in tiles:
                    last.then_inc(pv_done, 1)

            def turn_o(b, key, key_b, i, where=None):
                pe.wait_ge(o_evac, b.at(NI * b.n + i + 1, NI))
                bank = fill(key, key_b, where)
                for j in range(TJ):
                    last = nc.tensor.transpose(wk[:, bank, 0, j * P:j * P + P], o_sb[i % 2][:, j * P:j * P + P], ident[:, :])
                last.then_inc(wk_full[bank], 1)
                pe.wait_ge(wk_full[bank], slot(key, key_b, where)[1])
                pe.sem_inc(s_nt, 1)

            def project(b, k, where=None):
                pe.wait_ge(xtb[b.n % 2], b.at(16 * (b.n // 2 + 1), 8))
                for h in range(2):
                    m = 2 * k + h
                    n = ring(("QK"[k], h, b.n), None, where) if where else ring(("QK"[k], h), b.plus(-2))
                    wait(pe, st_free, n + 1 - ST_BANKS)
                    nc.tensor.matmul(st[:, n % ST_BANKS, :], w_sb[:, m * D:m * D + D], xTb[b.n % 2][:, :],
                                     start=True, stop=True).then_inc(st_full, 1)

            def project_v(b, key, key_b, where=None):
                pe.wait_ge(xtb[b.n % 2], b.at(16 * (b.n // 2 + 1), 8))
                bank = fill(key, key_b, where)
                for j in range(TJ):
                    last = nc.tensor.matmul(wk[:, bank, 0, j * D:j * D + D], xTb[b.n % 2][:, j * P:j * P + P],
                                            w_sb[:, 4 * D:5 * D], start=True, stop=True)
                last.then_inc(wk_full[bank], 1)

            def turn_attn(b, key_b, where=None):
                pe.wait_ge(attn_done, b.at(NI * (b.n + 1), NI))
                n = ring("AT", key_b, where)
                pe.wait_ge(st_free, n + 1 - ST_BANKS)
                for j in range(TJ):
                    last = nc.tensor.transpose(st[:, n % ST_BANKS, j * P:j * P + P], attn[b.n % 2][:, j, :], ident[:, :])
                last.then_inc(st_full, 1)
                pe.wait_ge(st_full, n + 1)
                pe.sem_inc(s_at, 1)

            def project_out(b, key_b, where=None):
                pe.wait_ge(st_free, ring("AT", key_b.plus(0) if key_b else None, where) + 1)
                bank = fill("OP", key_b, where)
                for j in range(TJ):
                    last = nc.tensor.matmul(wk[:, bank, 0, j * D:j * D + D], attnT[:, j * P:j * P + P], wo_sb[:, :],
                                            start=True, stop=True)
                last.then_inc(wk_full[bank], 1)
                pe.wait_ge(wk_full[bank], slot("OP", key_b, where)[1])
                pe.sem_inc(s_op, 1)

            def turn_x(b):
                pe.wait_ge(s_xn, TJ * (b + 1))
                bank = fill(("XT", b), None, "pro")
                for j in range(TJ):
                    last = nc.tensor.transpose(wk[:, bank, 0, j * P:j * P + P], xn[:, TJ * b + j, :], ident[:, :])
                last.then_inc(wk_full[bank], 1)

            pe.wait_ge(s_consts, 1)
            turn_x(0)
            turn_x(1)
            pe.wait_ge(s_c, N_CONST)
            for b in (Batch(0), Batch(1)):
                for k in range(2):
                    project(b, k, "pro")
                if b.n == 0:
                    project_v(b, ("V", 0), None, "pro")
            for b in range(2, NB):
                turn_x(b)
            bank = fill("GT", None, "pro")
            pe.wait_ge(s_xnT, NB)
            for t in range(NT):
                last = nc.tensor.matmul(wk[:, bank, 0, t * E:t * E + E], xnT[:, t * P:t * P + P], gw_sb[:, :],
                                        start=True, stop=True)
            last.then_inc(wk_full[bank], 1)
            pe.wait_ge(s_ones, 2)

            def wait_stack(b, i):
                pe.wait_ge(stacked[i], b.at(PIECES * (b.n + 1), PIECES))

            for i in range(NI):
                wait_stack(Batch(0), i)
                for pair in range(PAIRS):
                    scores(Batch(0), None, i, pair, "pro", (Batch(0), i - 1) if pair == 1 and i > 0 else None)

            bank = fill("CT", None, "pro")
            pe.wait_ge(f_either, 1)
            flat = either[:, :, :].rearrange("p t e -> p (t e)")
            nc.tensor.matmul(wk[:, bank, 0, 0:NT * E], ones, flat, start=True, stop=True)
            nc.tensor.matmul(wk[:, bank, 0, NT * E:2 * NT * E], above, flat, start=True, stop=True).then_inc(wk_full[bank], 1)

            def step(b):
                more, most = b.n + 1 < NB, b.n + 2 < NB
                b1, b2 = b.plus(1), b.plus(2)
                for i in range(NI):
                    prev, weighs = (b if i else b.plus(-1)), i > 0 or b.n > 0
                    if more:
                        wait_stack(b1, i)
                    for pair in range(PAIRS):
                        scores_t(b, i, pair)
                        turned = (b if i == 0 else b1, (i - 1) % NI) if pair == 1 else None
                        if more or pair == 1 and i == 0:
                            scores(b1, b, i, pair, None, turned)
                        if pair == 1 and weighs:
                            weigh(prev, (i - 1) % NI, (0,))
                        if pair == 2 and weighs:
                            weigh(prev, (i - 1) % NI, (1,))
                        if pair == 3 and weighs:
                            weigh(prev, (i - 1) % NI, (2, 3))
                        if pair == 3:
                            if i < 2 and most:
                                project(b2, i)
                            if i == 3 and b.n > 0:
                                project_out(b.plus(-1), b)
                        if pair == 4:
                            if i == 2 and b.n > 0:
                                turn_attn(b.plus(-1), b)
                        if pair == 5 and weighs:
                            turn_o(prev, ("N", i), b, (i - 1) % NI)
                        if pair == 5 and i == 3 and more:
                            project_v(b1, "V", b)

            def turn_xg(k):
                pe.wait_ge(f_xg[k.q], k.landed())
                wait(pe, f_xTs, k.plus(-1))
                nc.tensor.transpose(xT_ps[k.p][:, 0:P], xg[k.q][:, :], ident[:, :]).then_inc(f_xT, 1)

            def up(k):
                pe.wait_ge(f_w1, k.plus(1))
                pe.wait_ge(f_xTs, k.plus(1))
                wait(pe, f_gelu, k.plus(-1))
                for c in range(FC):
                    last = nc.tensor.matmul(h_ps[k.p][:, c * P:c * P + P], w1_e[k.p][:, c * P:c * P + P], xgT[k.p][:, :],
                                            start=True, stop=True)
                last.then_inc(f_up, 1)

            def down(k):
                pe.wait_ge(f_w2, k.plus(1))
                pe.wait_ge(f_gelu, k.plus(1))
                wait(pe, f_y, k.plus(-1))
                for c in range(FC):
                    last = nc.tensor.matmul(y_ps[k.p][:, 0:D], h[k.p][:, c, :], w2_e[k.p][:, c * D:c * D + D],
                                            start=c == 0, stop=c == FC - 1)
                last.then_inc(f_down, 1)

            def step_x(k, more):
                if more:
                    turn_xg(k.later(2))
                if k.turn is not None or k.n + 1 < BLOCKS:
                    up(k.later(1))
                down(k)

            def experts():
                pe.wait_ge(st_free, RING_START[EXPERTS_AT])
                pe.wait_ge(o_evac, NI * EXPERTS_AT - 1)
                for k in range(SLOTS):
                    pe.wait_ge(wk_free[k], len(range(k, START[EXPERTS_AT], SLOTS)))
                turn_xg(Block(0))
                turn_xg(Block(1))
                up(Block(0))
                blocks(pe, step_x, 2)
                experts_done(pe)

            loops(pe, step, experts)
            weigh(Batch(NB - 1), NI - 1, range(TJ))
            turn_o(Batch(NB - 1), "N", None, NI - 1, "epi")
            turn_attn(Batch(NB - 1), None, "epi")
            project_out(Batch(NB - 1), None, "epi")


def kernel(**inputs):
    import numpy as _np
    import concourse.bacc as _bacc
    from concourse import mybir as _mybir
    from concourse.bass_utils import run_bass_kernel_spmd as _run

    w = _np.asarray(inputs["L0_attn_qkv_w"])
    bias = _np.asarray(inputs["L0_attn_qkv_b"])
    turned = _np.arange(D).reshape(H, 2, HALF)[:, ::-1].reshape(D)
    wq, wk, wv = w[0:D], w[D:2 * D], w[2 * D:3 * D]
    bq, bk, bv = bias[0:D], bias[D:2 * D], bias[2 * D:3 * D]
    named = {
        "x": inputs["L0_attn_x"],
        "wqkv": _np.concatenate([wq, wq[turned], wk, wk[turned], wv]).T,
        "qkb": _np.stack([bq, bq[turned], bk, bk[turned]], 1),
        "vb": bv,
        "wo": _np.asarray(inputs["L0_attn_out_w"]).T,
        "ob": inputs["L0_attn_out_b"],
        "rope": rope_tables(),
        "gw": inputs["L0_ffn_gate_w"],
        "w1": _np.concatenate([_np.asarray(inputs["L0_ffn_w1"]).transpose(1, 0, 2),
                               _np.asarray(inputs["L0_ffn_b1"]).reshape(E, FC, P).transpose(2, 0, 1)], 2),
        "w2": _np.asarray(inputs["L0_ffn_w2"]).reshape(E, FC, P, D).transpose(2, 0, 1, 3),
        "b2": inputs["L0_ffn_b2"],
        "route": routing_tables(),
    }
    nc = _bacc.Bacc("TRN2", target_bir_lowering=False, num_devices=1)
    arrays, args = {}, []
    for name, a in named.items():
        a = _np.ascontiguousarray(a)
        arrays[f"in_{name}_dram"] = a
        args.append(nc.dram_tensor(f"in_{name}_dram", a.shape, _mybir.dt.from_np(a.dtype), kind="ExternalInput").ap())
    args.append(nc.dram_tensor("out_0_dram", (NB, S, D), _mybir.dt.float32, kind="ExternalOutput").ap())
    block_kernel(nc, *args)
    r = _run(nc, [arrays], core_ids=[0])
    return r.results[0]["out_0_dram"]
```

```python
import math
from contextlib import ExitStack

import numpy as np

import concourse.bass as bass
from concourse import mybir

F32 = mybir.dt.float32
F32R = mybir.dt.float32r
U32, I32 = mybir.dt.uint32, mybir.dt.int32
BF16 = mybir.dt.bfloat16
ALU = mybir.AluOpType
ACT = mybir.ActivationFunctionType
AX = mybir.AxisListType

NB, S, D = 8, 512, 128
H, HD = 16, 8
HALF = HD // 2
P = 128
TJ = S // P
NT = NB * TJ
G = 4
NI = H // G
E, F = 8, 512
EPS = 1e-5
SCALE = 1.0 / math.sqrt(HD)
NEG = -1e38
SLOTS = 2
ST_BANKS = 3
N_AT = 5
PAIRS = 6
CHUNKS = [[(0, 0, 512)], [(0, 1, 384)], [(0, 2, 256), (256, 3, 128)]]
CHUNK_AT, CHUNK_W = [0, 512, 896], [512, 384, 384]
PW = sum(CHUNK_W)
BLOCKS = (2 * NB * S + E * (P - 1)) // P + 1
TURN = 8
ROOM = 4
BLOCKS += -BLOCKS % TURN
FC = F // P
EXPERTS_AT = 4
SCATTERS = 5
GATHERS = 2 * NT // (NB - EXPERTS_AT) // NI
CLEAR = 6
PIECES = 5 * 16


def rope_tables():
    inv = (1.0 / 10000.0 ** (np.arange(HALF, dtype=np.float32) / np.float32(HALF))).astype(np.float32)
    angle = np.outer(np.arange(S, dtype=np.float32), inv).astype(np.float32)
    cos, sin = np.cos(angle).T, np.sin(angle).T
    cos8 = np.concatenate([cos, cos], 0)
    sin8 = np.concatenate([-sin, sin], 0)
    return np.tile(np.stack([cos8, sin8], 1), (H, 1, 1)).astype(np.float32)


def routing_tables():
    return np.concatenate([np.tile(np.arange(E, 0, -1), (P, 1)), np.tile(np.arange(BLOCKS), (P, 1)),
                           np.ones((P, P)), np.triu(np.ones((P, P)), 1)], 1).astype(np.float32)


def pair_at(at):
    return divmod(PAIRS - 1 - at, 3)


class Batch:

    def __init__(self, n, turn=None):
        self.n, self.turn = n, turn

    def at(self, count, each):
        return count if self.turn is None else self.turn * int(2 * each) + count

    def plus(self, k):
        return Batch(self.n + k, self.turn)






def slots_of(n):
    more, most = n + 1 < NB, n + 2 < NB
    extras = [("", False), ("", False), ("", False), ("OP", n > 0)]
    out = []
    for i in range(NI):
        pairs = [[("S", i, p)] if more else [] for p in range(PAIRS)]
        if not more and i == 0:
            pairs[1] = [("S", i, 1)]
        name, there = extras[i]
        nv = ([("N", i)] if i > 0 or n > 0 else []) + (["V"] if i == 3 and more else [])
        for p in range(PAIRS):
            if p == N_AT:
                out += nv
            out += pairs[p]
            if p == 3 and there:
                out.append(name)
    return out


def ring_of(n):
    out = []
    for i in range(NI):
        for pair in range(PAIRS):
            out += [("T", i, pair, h) for h in range(2)]
            if pair in (3, 4) and i < 2 and n + 2 < NB:
                out.append(("QK"[i], pair - 3))
            if pair == 4 and i == 2 and n > 0:
                out.append("AT")
    return out


RING_PRO = [("QK"[k], h, b) for b in range(2) for k in range(2) for h in range(2)]
RING_START = [len(RING_PRO)]
for _n in range(NB):
    RING_START.append(RING_START[-1] + len(ring_of(_n)))
RING_FULL = len(ring_of(1))


def ring(key, b=None, where=None):
    if where == "pro":
        return RING_PRO.index(key)
    if where == "epi":
        return RING_START[NB]
    return b.at(RING_START[b.n] + ring_of(b.n).index(key), RING_FULL)


def _s(i):
    return [("S", i, p) for p in range(PAIRS)]


PRO = [("XT", 0), ("XT", 1), ("V", 0), ("XT", 2), ("XT", 3)] + _s(0)
PRO += [("XT", b) for b in range(4, NB)] + ["GT"] + _s(1) + ["GL"] + _s(2) + ["CT"] + _s(3)
EPI = ["N", "OP"]
START = [len(PRO)]
for _n in range(NB):
    START.append(START[-1] + len(slots_of(_n)))
FULL = len(slots_of(1))
assert all(len(slots_of(n)) == FULL for n in range(1, NB - 2))


def slot(key, b=None, where=None):
    if where == "pro":
        s = PRO.index(key)
    elif where == "epi":
        s = START[NB] + EPI.index(key)
    else:
        s = START[b.n] + slots_of(b.n).index(key)
        return s % SLOTS, b.at(s // SLOTS + 1, FULL / SLOTS)
    return s % SLOTS, s // SLOTS + 1


def block_kernel(nc, x, wqkv, qkb, vb, wo, ob, rope, gw, w1, w2, b2, route, out):
    ctx = ExitStack()
    with ctx:
        def sb(name, shape, dt=F32):
            return ctx.enter_context(nc.sbuf_tensor(name, shape, dt))

        def sem(name):
            return ctx.enter_context(nc.semaphore(name))

        acc = sb("acc", [P, NT, D])
        xn_room = sb("xn_room", [P, E, F + FC])
        xn = xn_room[:, :, :].rearrange("p e f -> p (e f)")[:, 0:NT * D].rearrange("p (t d) -> p t d", d=D)
        logits = sb("logits", [P, NT, E])
        ident = sb("ident", [P, P])
        xnT = sb("xnT", [P, NB * S])
        stacks = [sb(f"stack{p}", [P, 2, NI, S], F32R) for p in range(2)]
        stack_q, stack_k = ([t[:, w] for t in stacks] for w in range(2))
        v32 = [sb(f"v32_{p}", [P, TJ, H, 32]) for p in range(2)]
        probs = [sb(f"probs{p}", [P, G, PW]) for p in range(2)]
        scratch = sb("scratch", [P, 6 * S])
        ev = scratch[:, 0:4 * S].rearrange("p (m t) -> p m t", m=4)
        qk = scratch[:, 4 * S:].rearrange("p (k t) -> p k t", k=2)
        halves = sb("halves", [P, 4, S], F32R)
        high, low = (halves[:, 2], halves[:, 1]), (halves[:, 0], halves[:, 3])
        rope_sb = sb("rope_sb", [P, 2, S])
        w_sb = sb("w_sb", [P, 5 * D])
        wo_sb = sb("wo_sb", [P, D])
        gw_sb = sb("gw_sb", [P, 32])
        qkb_sb = sb("qkb_sb", [P, 4])
        vb_sb = sb("vb_sb", [P, D])
        ob_sb = sb("ob_sb", [P, D])
        o_sb = [sb(f"o_sb{p}", [P, S]) for p in range(2)]
        attn = [sb(f"attn{p}", [P, TJ, D]) for p in range(2)]
        attnT = sb("attnT", [P, S])
        stats = sb("stats", [P, NT, 6])
        mv = sb("mv", [P, NT, 2])
        rstd = sb("rstd", [P, NT])
        half = sb("half", [P, TJ])
        part = [sb(f"part{p}", [P, G, 3]) for p in range(2)]
        nm = [sb(f"nm{p}", [P, G, TJ]) for p in range(2)]
        mrow = [sb(f"mrow{p}", [G * TJ, 2, P], F32R) for p in range(NI)]
        zeros = sb("zeros", [32, S], F32R)
        rec = sb("rec", [P, TJ, G])
        identb = sb("identb", [P, P], BF16)
        maskb = sb("maskb", [P, 5, P], BF16)

        w1_sb = xn_room
        w2_sb = probs[0][:, :, :].rearrange("p g w -> p (g w)").rearrange("p (e f) -> p e f", e=E)
        assert G * PW == E * (F + D)

        def parts(room, *shapes):
            views, at = [], 0
            for shape in shapes:
                n = math.prod(shape)
                v = room[:, at:at + n]
                views.append(v if len(shape) == 1 else v.rearrange("p (a b) -> p a b", a=shape[0]) if len(shape) == 2
                             else v.rearrange("p (a b c) -> p a b c", a=shape[0], b=shape[1]))
                at += n
            return views

        h, w1_e, xgT, y = parts(scratch, (2, FC, P), (2, F + FC), (2, P), (ROOM, D))
        h, w1_e, xgT, y = ([v[:, k] for k in range(v.shape[1])] for v in (h, w1_e, xgT, y))
        w2_e = [sb(f"w2_e{p}", [P, F + D]) for p in range(2)]
        xg = [sb(f"xg{p}", [P, D]) for p in range(ROOM)]
        YB = 4
        yg = sb("yg", [P, YB, D])
        share = sb("share", [P, 2, NT])
        place = sb("place", [P, 2, NT], U32)
        expert = sb("expert", [P, BLOCKS], I32)
        blocks_i = sb("blocks_i", [P, E], I32)
        gt = probs[0][:, :, :].rearrange("p g w -> p (g w)")[:, 0:2 * S].rearrange("p (a t) -> p a t", a=2)
        chosen, picked, lower, tmp, either, sums, beyond, blank, table, best, lead, ends, starts, expert_f, totals = parts(
            probs[1][:, :, :].rearrange("p g w -> p (g w)"), (2, NT, E), (2, NT, E), (NT, E), (NT, E), (NT, E), (4, NT, E), (BLOCKS, E),
            (6, D), (E + BLOCKS + 2 * P,), (2, NT), (NT,), (2, E), (E,), (BLOCKS,), (E,))
        sums, ends = [sums[:, k] for k in range(4)], [ends[:, k] for k in range(2)]
        prefer, number = table[:, 0:E], table[:, E:E + BLOCKS]
        ones, above = table[:, E + BLOCKS:E + BLOCKS + P], table[:, E + BLOCKS + P:]

        st = ctx.enter_context(nc.psum_tensor("st", [P, ST_BANKS, 512], F32))
        wk = ctx.enter_context(nc.psum_tensor("wk", [P, SLOTS, 2, 512], F32))
        po = ctx.enter_context(nc.psum_tensor("po", [P, 512], F32))

        h_ps, y_ps, xT_ps = [st[:, k] for k in range(2)], [st[:, 2], po], [wk[:, k, 0] for k in range(2)]

        xg_dram = nc.dram_tensor("xg_dram", (BLOCKS * P, D), F32, kind="Internal").ap()
        y_dram = nc.dram_tensor("y_dram", (BLOCKS * P, D), F32, kind="Internal").ap()
        out_v = out.rearrange("b (j p) d -> p (b j) d", p=P)

        w2_loaded = sem("w2_loaded")
        w1_loaded = sem("w1_loaded")
        blank_set = sem("blank_set")
        slots_cleared = sem("slots_cleared")
        routing_step = sem("routing_step")
        either_ready = sem("either_ready")
        lead_ready = sem("lead_ready")
        lead_exp_ready = sem("lead_exp_ready")
        places_ready = sem("places_ready")
        block_experts_ready = sem("block_experts_ready")
        tokens_scattered = sem("tokens_scattered")
        block_loaded = [sem(f"block_loaded{p}") for p in range(ROOM)]
        w1_copied = sem("w1_copied")
        w2_copied = sem("w2_copied")
        block_turned = sem("block_turned")
        xgT_ready = sem("xgT_ready")
        up_done = sem("up_done")
        gelu_done = sem("gelu_done")
        down_done = sem("down_done")
        y_ready = sem("y_ready")
        y_stored = [sem(f"y_stored{p}") for p in range(ROOM)]
        results_gathered = [sem(f"results_gathered{k}") for k in range(YB)]
        results_added = sem("results_added")
        out_stored = sem("out_stored")
        routing_loaded = sem("routing_loaded")
        counts_ready = sem("counts_ready")
        shares_ready = sem("shares_ready")
        starts_ready = sem("starts_ready")
        rank_step = sem("rank_step")
        ident_ready = sem("ident_ready")
        gate_scores_ready = sem("gate_scores_ready")
        logits_ready = sem("logits_ready")
        weights_loaded = sem("weights_loaded")
        rope_loaded = sem("rope_loaded")

        x_loaded = [sem(f"x_loaded{b}") for b in range(NB)]
        consts_loaded = sem("consts_loaded")
        ones_set = sem("ones_set")
        bn_stats_done = sem("bn_stats_done")
        variance_ready = sem("variance_ready")
        rstd_ready = sem("rstd_ready")
        xn_ready = sem("xn_ready")
        s_chain = sem("s_chain")
        pool_consts_set = sem("pool_consts_set")
        out_bias_added = sem("out_bias_added")
        xnT_ready = sem("xnT_ready")
        wk_full = [sem(f"wk_full{k}") for k in range(SLOTS)]
        wk_free = [sem(f"wk_free{k}") for k in range(SLOTS)]
        st_full = sem("st_full")
        st_free = sem("st_free")
        masked = sem("masked")
        pv_done = sem("pv_done")
        o_evac = sem("o_evac")
        v_ready = sem("v_ready")
        roped = sem("roped")
        split = sem("split")
        stacked = [sem(f"stacked{i}") for i in range(NI)]
        nm_done = sem("nm_done")
        mrow_done = sem("mrow_done")
        mstored = sem("mstored")
        mrows = [sem(f"mrows{i}") for i in range(NI)]
        attn_done = sem("attn_done")
        acc_done = sem("acc_done")
        zeros_set = sem("zeros_set")
        first_reduced = sem("first_reduced")
        rope_products = sem("rope_products")
        maxima_turned = sem("maxima_turned")
        v32_set = sem("v32_set")
        moments_ready = sem("moments_ready")
        high_ready = sem("high_ready")
        mrow_high_ready = sem("mrow_high_ready")
        reciprocals_ready = sem("reciprocals_ready")

        x_v = x.rearrange("b (j p) d -> p b j d", p=P)
        out_v = out.rearrange("b (j p) d -> p (b j) d", p=P)
        m_dram = nc.dram_tensor("m_dram", (NI, 2, G * TJ, P), F32, kind="Internal").ap()
        N_CONST = 4 * 16

        def wait(eng, s, v):
            if not (isinstance(v, int) and v <= 0):
                eng.wait_ge(s, v)

        def loops(eng, step, experts):
            for n in range(NB):
                if n == EXPERTS_AT:
                    experts()
                step(Batch(n))

        class Block:
            def __init__(self, n, turn=None):
                self.n, self.turn, self.p, self.q = n, turn, n % 2, n % ROOM

            def plus(self, v):
                return self.times(1, v)

            def times(self, v, c=0):
                return self.n * v + c if self.turn is None else self.turn * (TURN * v) + (self.n * v + c)

            def landed(self, c=0):
                v = 16 * (self.n // ROOM + 1 + c)
                return v if self.turn is None else self.turn * (16 * (TURN // ROOM)) + v

            def later(self, v):
                return Block(self.n + v, self.turn)

        def blocks(eng, body, ahead):
            for n in range(TURN):
                body(Block(n), True)
            with eng.Fori(1, BLOCKS // TURN - 1) as turn:
                for n in range(TURN):
                    body(Block(n, turn), True)
            for n in range(BLOCKS - TURN, BLOCKS):
                body(Block(n), n + ahead < BLOCKS)

        def expert_of(eng, k):
            at = k.plus(0)
            return eng.value_load(expert[0:1, at:at + 1] if isinstance(at, int) else expert[0:1, bass.ds(at, 1)],
                                  min_val=0, max_val=E - 1)

        def experts_stored(eng):
            for q in range(ROOM):
                eng.wait_ge(y_stored[q], 16 * (BLOCKS // ROOM))

        block = ctx.enter_context(nc.Block())

        @block.sync
        def _(sp):
            for b in range(NB):
                if b == 2:
                    sp.wait_ge(weights_loaded, 32)
                sp.dma_start(acc[:, TJ * b:TJ * b + TJ, :], x_v[:, b]).then_inc(x_loaded[b], 16)

            def stack(b, i):
                p = b.n % 2
                if b.n >= 2:
                    sp.wait_ge(st_full, ring(("T", i, PAIRS - 1, 1), b.plus(-2)) + 1)
                wait(sp, split, b.at(2 * b.n + 2, 2))
                wait(sp, stacked[i], b.at(PIECES * b.n, PIECES))
                src = slice(32 * i, 32 * i + 32)
                both = stacks[p][:, :, i, :]
                for dst, what in ((both[0:P:4, 0], halves[src, 2]), (both[0:P:4, 1], halves[src, 1]),
                                  (both[1:P:4], halves[src, 2:4]), (both[2:P:4], halves[src, 0:2]),
                                  (both[3:P:4, 0], zeros[:, :])):
                    sp.dma_start(dst.bitcast(F32), what.bitcast(F32)).then_inc(stacked[i], 16)

            def put_mrows(b, i):
                wait(sp, mrow_done, b.at(NI * b.n + i + 1, NI))
                sp.dma_start(m_dram[i].rearrange("r (g j) t -> (g j) r t", g=G),
                             mrow[i][:, :, :].bitcast(F32)).then_inc(mstored, 16)
                sp.wait_ge(mstored, b.at(16 * (NI * b.n + i + 1), 16 * NI))
                wait(sp, mrows[i], b.at(32 * b.n, 32))
                sp.wait_ge(stacked[i], b.at(PIECES * (b.n + 1), PIECES))
                for r in range(2):
                    sp.dma_start(stack_q[b.n % 2][3 + 4 * r:P:32, i, :].bitcast(F32),
                                 m_dram[i, r].rearrange("(g j) t -> g (j t)", g=G)).then_inc(mrows[i], 16)

            sp.wait_ge(zeros_set, 1)
            sp.wait_ge(ones_set, 2)
            for i in range(NI):
                stack(Batch(0), i)
            sp.wait_ge(blank_set, 1)
            for k in range(0, BLOCKS, CLEAR):
                sp.dma_start(xg_dram[k * P:(k + CLEAR) * P, :].rearrange("(k p) d -> p k d", p=P),
                             blank[:, :, :]).then_inc(slots_cleared, 16)
            put_mrows(Batch(0), 0)
            for i in range(NI):
                stack(Batch(1), i)
            for i in range(1, NI - 1):
                put_mrows(Batch(0), i)

            def load(k):
                wait(sp, block_turned, k.plus(1 - ROOM))
                at = k.times(P)
                src = xg_dram[at:at + P, :] if isinstance(at, int) else xg_dram[bass.ds(at, P), :]
                sp.dma_start(xg[k.q][:, :], src).then_inc(block_loaded[k.q], 16)

            def step(b):
                for i in range(NI):
                    if b.n == EXPERTS_AT - 1 and i == NI - 2:
                        sp.wait_ge(tokens_scattered, 16 * 2 * NT)
                        for n in range(ROOM):
                            load(Block(n))
                    if i == 0:
                        put_mrows(b, NI - 1)
                    elif b.n + 1 < NB:
                        put_mrows(b.plus(1), i - 1)
                    if b.n + 2 < NB:
                        stack(b.plus(2), i)

            def experts():
                blocks(sp, step_x, ROOM)
                store(Block(BLOCKS - 2))
                store(Block(BLOCKS - 1))

            def store(k):
                sp.wait_ge(y_ready, k.plus(1))
                at = k.times(P)
                dst = y_dram[at:at + P, :] if isinstance(at, int) else y_dram[bass.ds(at, P), :]
                sp.dma_start(dst, y[k.q][:, :]).then_inc(y_stored[k.q], 16)

            def step_x(k, more):
                if more:
                    load(k.later(ROOM))
                if k.turn is not None or k.n >= 2:
                    store(k.later(-2))

            loops(sp, step, experts)
            sp.wait_ge(results_added, 2 * NT)
            sp.wait_ge(acc_done, NB - 1)
            last = TJ * (NB - 1)
            sp.dma_start(out_v[:, 0:last, :], acc[:, 0:last, :]).then_inc(out_stored, 16)
            sp.wait_ge(acc_done, NB)
            sp.dma_start(out_v[:, last:, :], acc[:, last:, :]).then_inc(out_stored, 16)
            sp.wait_ge(out_stored, 32)

        @block.gpsimd
        def _(pool):
            nc.gpsimd.memset(ident[:, :], 0.0).then_inc(pool_consts_set, 1)
            nc.gpsimd.memset(half[:, :], -0.5).then_inc(pool_consts_set, 1)
            pool.wait_ge(pool_consts_set, 2)
            nc.gpsimd.affine_select(out=ident[:, :], in_=ident[:, :], pattern=[[-1, P]], compare_op=ALU.not_equal,
                                    fill=1.0, base=0, channel_multiplier=1).then_inc(ident_ready, 1)

            def root(b):
                pool.wait_ge(variance_ready, b + 1)
                nc.gpsimd.tensor_tensor(rstd[:, TJ * b:TJ * b + TJ], rstd[:, TJ * b:TJ * b + TJ], half[:, :],
                                        ALU.pow).then_inc(rstd_ready, 1)

            root(0)
            nc.gpsimd.memset(maskb[:, :, :], 0.0).then_inc(pool_consts_set, 1)
            pool.wait_ge(pool_consts_set, 3)
            nc.gpsimd.affine_select(out=maskb[:, 3:5, :], in_=maskb[:, 3:5, :], pattern=[[0, 2], [-1, P]],
                                    compare_op=ALU.is_ge, fill=NEG, base=0, channel_multiplier=1).then_inc(pool_consts_set, 1)
            pool.wait_ge(ident_ready, 1)
            nc.gpsimd.tensor_copy(identb[:, :], ident[:, :]).then_inc(pool_consts_set, 1)
            root(1)
            nc.gpsimd.memset(blank[:, :, :], 0.0).then_inc(blank_set, 1)
            nc.gpsimd.memset(zeros[:, :].bitcast(F32), 0.0).then_inc(zeros_set, 1)
            root(2)
            for t in stack_k:
                nc.gpsimd.memset(t.bitcast(F32), 1.0).then_inc(ones_set, 1)
            root(3)
            pool.wait_ge(rope_loaded, 16)

            def rope_qk(b, k):
                key = ("QK"[k], 1)
                pool.wait_ge(st_free, (ring(key, b.plus(-2)) if b.n > 1 else ring((*key, b.n), None, "pro")) + 1)
                wait(pool, split, b.at(2 * b.n, 2))
                a_, b_ = ev[:, 2 * k], ev[:, 2 * k + 1]
                nc.gpsimd.tensor_tensor(a_, a_, rope_sb[:, 0], ALU.mult).then_inc(rope_products, 1)
                nc.gpsimd.tensor_tensor(b_, b_, rope_sb[:, 1], ALU.mult).then_inc(rope_products, 1)
                pool.wait_ge(rope_products, b.at(4 * b.n + 2 * k + 2, 4))
                nc.gpsimd.tensor_tensor(qk[:, k], a_, b_, ALU.add).then_inc(roped, 1)

            root(4)
            root(5)
            root(6)
            root(7)
            rope_qk(Batch(1), 0)
            rope_qk(Batch(1), 1)
            pool.wait_ge(consts_loaded, N_CONST)
            for b in range(NB):
                pool.wait_ge(xn_ready, TJ * (b + 1))
                t = acc[:, TJ * b:TJ * b + TJ, :]
                nc.gpsimd.tensor_tensor(t, t, ob_sb[:, :].unsqueeze(1).to_broadcast([P, TJ, D]), ALU.add).then_inc(out_bias_added, 1)

            links = [0]

            def link(ins):
                links[0] += 1
                ins.then_inc(rank_step, 1)
                pool.wait_ge(rank_step, links[0])

            pool.wait_ge(counts_ready, 2)
            a, step, upto = 0, 1, sums[2]
            while step < NT:
                nc.gpsimd.tensor_copy(sums[a][:, 0:step, :], upto[:, 0:step, :])
                link(nc.gpsimd.tensor_tensor(sums[a][:, step:, :], upto[:, step:, :], upto[:, :NT - step, :], ALU.add))
                upto, a, step = sums[a], 1 - a, 2 * step
            rank = sums[a]
            link(nc.gpsimd.tensor_tensor(rank[:, :, :], upto[:, :, :], sums[2][:, :, :], ALU.subtract))
            link(nc.gpsimd.tensor_tensor(rank[:, :, :], rank[:, :, :], sums[3][:, :, :], ALU.add))
            pool.wait_ge(starts_ready, 1)
            link(nc.gpsimd.tensor_tensor(rank[:, :, :], rank[:, :, :], starts[:, :].unsqueeze(1).to_broadcast([P, NT, E]), ALU.add))
            for c in range(2):
                link(nc.gpsimd.tensor_tensor(picked[:, c], rank[:, :, :], chosen[:, c], ALU.mult))
            width = E
            while width > 1:
                width //= 2
                link(nc.gpsimd.tensor_tensor(picked[:, :, :, 0:width], picked[:, :, :, 0:width],
                                             picked[:, :, :, width:2 * width], ALU.add))
            nc.gpsimd.tensor_copy(place[:, :, :], picked[:, :, :, 0]).then_inc(places_ready, 1)

            def scatter(n):
                t, c = divmod(n, 2)
                nc.gpsimd.indirect_dma_start(xg_dram[:, :], bass.IndirectOffsetOnAxis(place[:, c, t:t + 1], 0),
                                             xn[:, t, :], None).then_inc(tokens_scattered, 16)

            def gather(n):
                t, c = divmod(n, 2)
                wait(pool, results_added, n - YB + 1)
                nc.gpsimd.indirect_dma_start(yg[:, n % YB, :], None, y_dram[:, :],
                                             bass.IndirectOffsetOnAxis(place[:, c, t:t + 1], 0)).then_inc(results_gathered[n % YB], 16)

            def step(b):
                for i in range(NI):
                    gpar = i % 2
                    period = NI * b.n + i
                    for u in range(PAIRS):
                        c, gp = u % 3, u // 3
                        pool.wait_ge(st_free, ring(("T", i, u, 1), b) + 1)
                        at = CHUNK_AT[c]
                        if c < 2:
                            v = probs[gpar][:, 2 * gp:2 * gp + 2, at:at + P]
                            pat = [[0, 2], [1, P]]
                            nc.gpsimd.affine_select(out=v, in_=v, pattern=pat, compare_op=ALU.is_ge, fill=0.0,
                                                    base=0, channel_multiplier=-1).then_inc(masked, 1)
                        else:
                            for k in range(2):
                                v = probs[gpar][:, 2 * gp:2 * gp + 2, at + 256 * k:at + 256 * k + P]
                                last = nc.gpsimd.affine_select(out=v, in_=v, pattern=[[0, 2], [1, P]],
                                                               compare_op=ALU.is_ge, fill=0.0, base=0,
                                                               channel_multiplier=-1)
                                last.then_inc(masked, 1)
                    if i < 2 and b.n + 2 < NB:
                        rope_qk(b.plus(2), i)
                    if b.n < EXPERTS_AT:
                        if period == 0:
                            pool.wait_ge(places_ready, 1)
                            pool.wait_ge(slots_cleared, 16 * (BLOCKS // CLEAR))
                        for n in range(SCATTERS * period, min(SCATTERS * (period + 1), 2 * NT)):
                            scatter(n)
                    else:
                        for n in range(GATHERS):
                            gather(GATHERS * (period - NI * EXPERTS_AT) + n)

            loops(pool, step, lambda: experts_stored(pool))

        @block.scalar
        def _(act):
            def evac_qk(b, k, where=None, halves=range(2)):
                wait(act, roped, b.at(2 * (b.n - 1) + k + 1, 2))
                if b.n == EXPERTS_AT + 2:
                    experts_stored(act)
                for h in halves:
                    n = ring(("QK"[k], h, b.n), None, where) if where else ring(("QK"[k], h), b.plus(-2))
                    m = 2 * k + h
                    act.wait_ge(st_full, n + 1)
                    nc.scalar.activation(ev[:, m], st[:, n % ST_BANKS, :], ACT.Identity, bias=qkb_sb[:, m:m + 1]).then_inc(st_free, 1)

            def evac_plain(key, b, where, dst, done, count):
                w, n = slot(key, b, where)
                act.wait_ge(wk_full[w], n)
                nc.scalar.activation(dst, wk[:, w, 0, :], ACT.Copy).then_inc(done, 1)
                act.wait_ge(done, count)
                act.sem_inc(wk_free[w], 1)

            nc.scalar.dma_start(w_sb[:, :], wqkv).then_inc(weights_loaded, 16)
            nc.scalar.dma_start(qkb_sb[:, :], qkb).then_inc(weights_loaded, 16)
            nc.scalar.dma_start(rope_sb[:, :, :], rope).then_inc(rope_loaded, 16)
            nc.scalar.dma_start(vb_sb[:, :], vb.partition_broadcast(P)).then_inc(consts_loaded, 16)
            nc.scalar.dma_start(gw_sb[:, :], gw).then_inc(consts_loaded, 16)
            nc.scalar.dma_start(ob_sb[:, :], ob.partition_broadcast(P)).then_inc(consts_loaded, 16)
            nc.scalar.dma_start(wo_sb[:, :], wo).then_inc(consts_loaded, 16)
            nc.scalar.dma_start(table[:, :], route).then_inc(routing_loaded, 16)
            for b in range(2):
                evac_plain(("XT", b), None, "pro", xnT[:, S * b:S * b + S], xnT_ready, b + 1)
            act.wait_ge(weights_loaded, 32)
            for b in range(2):
                evac_qk(Batch(b), 0, "pro")
                evac_qk(Batch(b), 1, "pro")
            for b in range(2, NB):
                evac_plain(("XT", b), None, "pro", xnT[:, S * b:S * b + S], xnT_ready, b + 1)

            def evac_o(b, i):
                act.wait_ge(pv_done, b.at(NI * b.n + i + 1, NI))
                if NI * b.n + i >= 2:
                    of, at = divmod(NI * b.n + i - 1, NI)
                    w, n = slot(("N", at), Batch(of))
                    act.wait_ge(wk_full[w], n)
                nc.scalar.activation(o_sb[i % 2][:, :], po[:, :], ACT.Copy).then_inc(o_evac, 1)

            def evac_at(b, key_b, where):
                if b.n > 0:
                    w, n = slot("OP", b)
                    act.wait_ge(wk_full[w], n)
                n = ring("AT", key_b, where)
                act.wait_ge(st_full, n + 1)
                nc.scalar.activation(attnT[:, :], st[:, n % ST_BANKS, :], ACT.Copy).then_inc(st_free, 1)

            def exps(b, i, pair):
                gp, c = divmod(pair, 3)
                group = NI * b.n + i
                if pair == 0:
                    wait(act, pv_done, b.at(group - 1, NI))
                if pair == 0 and group == 1:
                    act.wait_ge(shares_ready, 1)
                    act.wait_ge(places_ready, 1)
                    act.wait_ge(slots_cleared, 16 * (BLOCKS // CLEAR))
                at, w = CHUNK_AT[c], CHUNK_W[c]
                for h in range(2):
                    n = ring(("T", i, pair, h), b)
                    act.wait_ge(st_full, n + 1)
                    nc.scalar.activation(probs[i % 2][:, 2 * gp + h, at:at + w], st[:, n % ST_BANKS, 0:w],
                                         ACT.Exp, scale=SCALE).then_inc(st_free, 1)

            def step(b):
                most = b.n + 2 < NB
                for i in range(NI):
                    if b.n == EXPERTS_AT - 1 and i == 2:
                        act.wait_ge(tokens_scattered, 16 * 2 * NT)
                        nc.scalar.dma_start(w1_sb[:, :, :], w1).then_inc(w1_loaded, 16)
                    exps(b, i, 0)
                    exps(b, i, 1)
                    exps(b, i, 2)
                    if i > 0 or b.n > 0:
                        evac_o(b if i else b.plus(-1), (i - 1) % NI)
                    if b.n == EXPERTS_AT - 1 and i == 3:
                        nc.scalar.dma_start(w2_sb[:, :, 0:F], w2).then_inc(w2_loaded, 16)
                        nc.scalar.dma_start(w2_sb[:, :, F:], b2.partition_broadcast(P)).then_inc(w2_loaded, 16)
                    exps(b, i, 3)
                    if i < 2 and most:
                        evac_qk(b.plus(2), i, halves=(0,))
                    exps(b, i, 4)
                    if i < 2 and most:
                        evac_qk(b.plus(2), i, halves=(1,))
                    if i == 2 and b.n > 0:
                        evac_at(b.plus(-1), b, None)
                    exps(b, i, 5)

            def turn(k):
                act.wait_ge(block_turned, k.plus(1))
                wait(act, up_done, k.plus(-1))
                nc.scalar.activation(xgT[k.p][:, :], xT_ps[k.p][:, 0:P], ACT.Copy).then_inc(xgT_ready, 1)

            def gelu(k):
                act.wait_ge(up_done, k.plus(1))
                act.wait_ge(w1_copied, k.plus(1))
                wait(act, down_done, k.plus(-1))
                for c in range(FC):
                    last = nc.scalar.activation(h[k.p][:, c, :], h_ps[k.p][:, c * P:c * P + P], ACT.Gelu,
                                                bias=w1_e[k.p][:, F + c:F + c + 1])
                last.then_inc(gelu_done, 1)

            def step_x(k, more):
                if more:
                    turn(k.later(2))
                if k.turn is not None or k.n + 1 < BLOCKS:
                    gelu(k.later(1))

            def experts():
                act.wait_ge(split, 2 * (EXPERTS_AT + 2))
                turn(Block(0))
                turn(Block(1))
                gelu(Block(0))
                blocks(act, step_x, 2)
                act.wait_ge(y_ready, BLOCKS)

            w, n = slot("GT", None, "pro")
            act.wait_ge(wk_full[w], n)
            nc.scalar.activation(gt[:, :, :], wk[:, w], ACT.Copy).then_inc(gate_scores_ready, 1)
            act.wait_ge(gate_scores_ready, 1)
            act.sem_inc(wk_free[w], 1)
            act.wait_ge(lead_ready, 1)
            nc.scalar.activation(lead[:, :], lead[:, :], ACT.Exp).then_inc(lead_exp_ready, 1)
            loops(act, step, experts)
            evac_o(Batch(NB - 1), NI - 1)
            evac_at(Batch(NB - 1), None, "epi")


        @block.vector
        def _(dve):
            for t in v32:
                nc.vector.memset(t[:, :, :, :], 0.0).then_inc(v32_set, 1)
            dve.wait_ge(v32_set, 2)
            for t in v32:
                nc.vector.memset(t[:, :, :, HD:HD + 1], 1.0).then_inc(v32_set, 1)
            def measure(b):
                dve.wait_ge(x_loaded[b], 16)
                for t in range(TJ * b, TJ * b + TJ):
                    nc.vector.bn_stats(stats[:, t, :], acc[:, t, :]).then_inc(bn_stats_done, 1)
                dve.wait_ge(bn_stats_done, TJ * (b + 1))
                for t in range(TJ * b, TJ * b + TJ):
                    nc.vector.bn_aggr(mv[:, t, :], stats[:, t, :]).then_inc(moments_ready, 1)
                dve.wait_ge(moments_ready, TJ * (b + 1))
                nc.vector.tensor_scalar_add(rstd[:, TJ * b:TJ * b + TJ], mv[:, TJ * b:TJ * b + TJ, 1],
                                            EPS).then_inc(variance_ready, 1)

            def normalise(b):
                dve.wait_ge(rstd_ready, b + 1)
                for t in range(TJ * b, TJ * b + TJ):
                    nc.vector.tensor_scalar(xn[:, t, :], acc[:, t, :], mv[:, t, 0:1], rstd[:, t:t + 1],
                                            ALU.subtract, ALU.mult).then_inc(xn_ready, 1)

            def rope_qk(b, k):
                key = ("QK"[k], 1)
                dve.wait_ge(st_free, (ring(key, b.plus(-2)) if b.n > 1 else ring((*key, b.n), None, "pro")) + 1)
                wait(dve, split, b.at(2 * b.n, 2))
                a_, b_ = ev[:, 2 * k], ev[:, 2 * k + 1]
                nc.vector.tensor_tensor(a_, a_, rope_sb[:, 0], ALU.mult).then_inc(rope_products, 1)
                nc.vector.tensor_tensor(b_, b_, rope_sb[:, 1], ALU.mult).then_inc(rope_products, 1)
                dve.wait_ge(rope_products, b.at(4 * b.n + 2 * k + 2, 4))
                nc.vector.tensor_tensor(qk[:, k], a_, b_, ALU.add).then_inc(roped, 1)

            def split_qk(b, k):
                dve.wait_ge(roped, b.at(2 * b.n + k + 1, 2))
                for p in range(NI):
                    wait(dve, stacked[p], b.at(PIECES * b.n, PIECES))
                nc.vector.tensor_copy(high[k], qk[:, k]).then_inc(high_ready, 1)
                dve.wait_ge(high_ready, b.at(2 * b.n + k + 1, 2))
                nc.vector.tensor_tensor(low[k], qk[:, k], high[k].bitcast(F32), ALU.subtract).then_inc(split, 1)

            def put_v(b, key, key_b, where):
                bank, n = slot(key, key_b, where)
                dve.wait_ge(wk_full[bank], n)
                wait(dve, pv_done, b.at(NI * (b.n - 1), NI))
                src = wk[:, bank, 0, :].rearrange("p (j h d) -> p j h d", j=TJ, h=H)
                bias = vb_sb[:, :].rearrange("p (h d) -> p h d", h=H).unsqueeze(1).to_broadcast([P, TJ, H, HD])
                nc.vector.tensor_tensor(v32[b.n % 2][:, :, :, 0:HD], src, bias, ALU.add).then_inc(v_ready, 1)
                dve.wait_ge(v_ready, b.at(b.n + 1, 1))
                dve.sem_inc(wk_free[bank], 1)

            def maxima(b, key_b, i, at, where=None, turns=False):
                gp, c = pair_at(at)
                if at == 0:
                    wait(dve, maxima_turned, b.at(NI * b.n + i - 1, NI))
                w, n = slot(("S", i, at), key_b, where)
                dve.wait_ge(wk_full[w], n)
                g = slice(2 * gp, 2 * gp + 2)
                if c == 0:
                    dst, src = part[i % 2][:, g, :], wk[:, w, :, 0:3 * P].rearrange("p h (u k) -> p h u k", u=3)
                else:
                    dst, src = nm[i % 2][:, g, c + 1], wk[:, w, :, 0:(c + 2) * P]
                if turns:
                    nc.vector.tensor_reduce(dst, src, AX.X, ALU.max, negate=True).then_inc(first_reduced, 1)
                else:
                    nc.vector.tensor_reduce(dst, src, AX.X, ALU.max, negate=True).then_inc(wk_free[w], 1)
                if at == PAIRS - 1:
                    dve.wait_ge(wk_free[w], n)
                    nc.vector.tensor_copy(nm[i % 2][:, :, 0], part[i % 2][:, :, 0]).then_inc(nm_done, 1)
                    nc.vector.tensor_tensor(nm[i % 2][:, :, 1], part[i % 2][:, :, 1], part[i % 2][:, :, 2],
                                            ALU.min).then_inc(nm_done, 1)

            def max_rows(b, key, key_b, i, where):
                w, n = slot(key, key_b, where)
                dve.wait_ge(wk_full[w], n)
                wait(dve, mrows[i], b.at(32 * b.n, 32))
                src = wk[0:G * TJ, w, 0, 3 * P:4 * P]
                nc.vector.tensor_copy(mrow[i][:, 0, :], src).then_inc(mrow_high_ready, 1)
                dve.wait_ge(mrow_high_ready, b.at(NI * b.n + i + 1, NI))
                nc.vector.tensor_tensor(mrow[i][:, 1, :], src, mrow[i][:, 0, :].bitcast(F32),
                                        ALU.subtract).then_inc(mrow_done, 1)
                dve.wait_ge(mrow_done, b.at(NI * b.n + i + 1, NI))
                dve.sem_inc(wk_free[w], 1)

            def norm(b, key, key_b, i, where=None):
                bank, n = slot(key, key_b, where)
                dve.wait_ge(wk_full[bank], n)
                src = wk[:, bank, 0, :].rearrange("p (j g c) -> p j g c", j=TJ, g=G)
                nc.vector.reciprocal(rec[:, :, :], src[:, :, :, HD]).then_inc(reciprocals_ready, 1)
                dve.wait_ge(reciprocals_ready, b.at(NI * b.n + i + 1, NI))
                if i == 0:
                    if b.n > 1:
                        dve.wait_ge(st_full, ring("AT", b.plus(-1)) + 1)
                dst = attn[b.n % 2][:, :, 32 * i:32 * i + 32].rearrange("p j (g d) -> p j g d", g=G)
                nc.vector.tensor_tensor(dst, src[:, :, :, 0:HD], rec[:, :, :].unsqueeze(3).to_broadcast([P, TJ, G, HD]),
                                        ALU.mult).then_inc(attn_done, 1)
                dve.wait_ge(attn_done, b.at(NI * b.n + i + 1, NI))
                dve.sem_inc(wk_free[bank], 1)

            def add_out(b, key_b, where=None):
                bank, n = slot("OP", key_b, where)
                dve.wait_ge(wk_full[bank], n)
                wait(dve, results_added, GATHERS * (NI * (b.n + 1 - EXPERTS_AT) + 2) if key_b else 2 * NT)
                row = b.at(TJ * b.n, TJ)
                t = acc[:, row:row + TJ, :] if isinstance(row, int) else acc[:, bass.ds(row, TJ), :]
                nc.vector.tensor_tensor(t, wk[:, bank, 0, :].rearrange("p (j d) -> p j d", j=TJ), t,
                                        ALU.add).then_inc(acc_done, 1)
                dve.wait_ge(acc_done, b.at(b.n + 1, 1))
                dve.sem_inc(wk_free[bank], 1)

            b0, b1 = Batch(0), Batch(1)
            measure(0)
            measure(1)
            normalise(0)
            measure(2)
            normalise(1)
            measure(3)
            normalise(2)
            measure(4)
            normalise(3)
            dve.wait_ge(rope_loaded, 16)
            rope_qk(b0, 0)
            split_qk(b0, 0)
            rope_qk(b0, 1)
            split_qk(b0, 1)
            dve.wait_ge(consts_loaded, N_CONST)
            put_v(b0, ("V", 0), None, "pro")
            measure(5)
            normalise(4)
            measure(6)
            normalise(5)
            measure(7)
            normalise(6)
            normalise(7)

            def first_maxima(i, places=range(PAIRS)):
                for pair in places:
                    turns = pair == 1 and i > 0
                    maxima(b0, None, i, pair, "pro", turns)
                    if turns:
                        dve.wait_ge(first_reduced, i)
                        max_rows(b0, ("S", i, 1), None, i - 1, "pro")

            first_maxima(0)
            split_qk(b1, 0)
            first_maxima(1)
            split_qk(b1, 1)
            bank, n = slot("GL", None, "pro")
            dve.wait_ge(wk_full[bank], n)
            for half in range(2):
                nc.vector.tensor_copy(logits[:, half * NT // 2:(half + 1) * NT // 2, :].rearrange("p (b j) e -> p b j e", j=TJ),
                                      wk[:, bank, half, :].rearrange("p (j b x) -> p b j x", j=TJ, b=4)[:, :, :, 0:E]).then_inc(logits_ready, 1)
            dve.wait_ge(logits_ready, 2)
            dve.sem_inc(wk_free[bank], 1)
            dve.wait_ge(out_bias_added, NB)
            links = [0]

            def link(ins):
                links[0] += 1
                ins.then_inc(routing_step, 1)
                dve.wait_ge(routing_step, links[0])

            def along_e(v):
                return v.unsqueeze(2).to_broadcast([P, NT, E])

            prefers = prefer.unsqueeze(1).to_broadcast([P, NT, E])
            dve.wait_ge(routing_loaded, 16)
            scores = logits
            def choose(c, scores):
                link(nc.vector.tensor_reduce(best[:, c], scores[:, :, :], AX.X, ALU.max))
                link(nc.vector.tensor_tensor(tmp[:, :, :], scores[:, :, :], along_e(best[:, c]), ALU.is_equal))
                link(nc.vector.tensor_tensor(tmp[:, :, :], tmp[:, :, :], prefers, ALU.mult))
                link(nc.vector.tensor_reduce(share[:, c], tmp[:, :, :], AX.X, ALU.max))
                link(nc.vector.tensor_tensor(chosen[:, c], prefers, along_e(share[:, c]), ALU.is_equal))

            choose(0, logits)
            link(nc.vector.scalar_tensor_tensor(lower[:, :, :], chosen[:, 0], -3e38, logits[:, :, :], ALU.mult, ALU.add))
            first_maxima(2, range(3))
            choose(1, lower)
            nc.vector.tensor_tensor(either[:, :, :], chosen[:, 0], chosen[:, 1], ALU.add).then_inc(either_ready, 1)
            nc.vector.tensor_tensor(lead[:, :], best[:, 1], best[:, 0], ALU.subtract).then_inc(lead_ready, 1)
            first_maxima(2, range(3, PAIRS))

            bank, n = slot("CT", None, "pro")
            dve.wait_ge(wk_full[bank], n)
            for k in range(2):
                nc.vector.tensor_copy(sums[2 + k][:, :, :], wk[:, bank, 0, k * NT * E:(k + 1) * NT * E].rearrange(
                    "p (t e) -> p t e", e=E)).then_inc(counts_ready, 1)
            dve.wait_ge(counts_ready, 2)
            dve.sem_inc(wk_free[bank], 1)
            link(nc.vector.tensor_reduce(totals[:, :], sums[2][:, :, :].rearrange("p t e -> p e t"), AX.X, ALU.add))
            link(nc.vector.tensor_scalar(blocks_i[:, :], totals[:, :], float(P - 1), None, ALU.add))
            link(nc.vector.tensor_scalar(blocks_i[:, :], blocks_i[:, :], int(math.log2(P)), None, ALU.arith_shift_right))
            link(nc.vector.tensor_copy(ends[0][:, :], blocks_i[:, :]))
            link(nc.vector.tensor_copy(starts[:, :], ends[0][:, :]))
            b, step = 0, 1
            while step < E:
                nc.vector.tensor_copy(ends[1 - b][:, 0:step], ends[b][:, 0:step])
                link(nc.vector.tensor_tensor(ends[1 - b][:, step:], ends[b][:, step:], ends[b][:, :E - step], ALU.add))
                b, step = 1 - b, 2 * step
            link(nc.vector.tensor_tensor(starts[:, :], ends[b][:, :], starts[:, :], ALU.subtract))
            nc.vector.tensor_scalar(starts[:, :], starts[:, :], float(P), None, ALU.mult).then_inc(starts_ready, 1)
            first_maxima(3)
            link(nc.vector.tensor_tensor(beyond[:, :, :], number.unsqueeze(2).to_broadcast([P, BLOCKS, E]),
                                         ends[b][:, :].unsqueeze(1).to_broadcast([P, BLOCKS, E]), ALU.is_ge))
            link(nc.vector.tensor_reduce(expert_f[:, :], beyond[:, :, :], AX.X, ALU.add))
            nc.vector.tensor_scalar(expert[:, :], expert_f[:, :], float(E - 1), None, ALU.min).then_inc(block_experts_ready, 1)
            dve.wait_ge(lead_exp_ready, 1)
            link(nc.vector.tensor_scalar(share[:, 1], lead[:, :], 1.0, None, ALU.add))
            link(nc.vector.reciprocal(share[:, 0], share[:, 1]))
            nc.vector.tensor_tensor(share[:, 1], share[:, 0], lead[:, :], ALU.mult).then_inc(shares_ready, 1)
            dve.wait_ge(block_experts_ready, 1)


            def copy_w1(k, e):
                wait(dve, gelu_done, k.plus(-1))
                nc.vector.tensor_copy(w1_e[k.p][:, :], w1_sb[:, bass.ds(e, 1), :].squeeze(1)).then_inc(w1_copied, 1)

            def copy_w2(k, e):
                wait(dve, y_ready, k.plus(-1))
                nc.vector.tensor_copy(w2_e[k.p][:, :], w2_sb[:, bass.ds(e, 1), :].squeeze(1)).then_inc(w2_copied, 1)

            def finish(k):
                dve.wait_ge(down_done, k.plus(1))
                wait(dve, y_stored[k.q], k.landed(-1))
                nc.vector.tensor_tensor(y[k.q][:, :], y_ps[k.p][:, 0:D], w2_e[k.p][:, F:], ALU.add).then_inc(y_ready, 1)

            def step_x(k, more):
                if more:
                    e = expert_of(dve, k.later(2))
                    copy_w1(k.later(2), e)
                finish(k)
                if more:
                    copy_w2(k.later(2), e)


            def experts():
                dve.wait_ge(split, 2 * (EXPERTS_AT + 2))
                dve.wait_ge(w1_loaded, 16)
                first = [(k, expert_of(dve, k)) for k in (Block(0), Block(1))]
                for k, e in first:
                    copy_w1(k, e)
                dve.wait_ge(w2_loaded, 2 * 16)
                for k, e in first:
                    copy_w2(k, e)
                blocks(dve, step_x, 2)

            def add_expert(n):
                t, c = divmod(n, 2)
                dve.wait_ge(results_gathered[n % YB], 16 * (n // YB + 1))
                wait(dve, results_added, n)
                nc.vector.scalar_tensor_tensor(acc[:, t, :], yg[:, n % YB, :], share[:, c, t:t + 1], acc[:, t, :],
                                               ALU.mult, ALU.add).then_inc(results_added, 1)

            def step(b):
                more, most = b.n + 1 < NB, b.n + 2 < NB
                for i in range(NI):
                    for pair in range(PAIRS):
                        if pair == N_AT and (i > 0 or b.n > 0):
                            norm(b if i else b.plus(-1), ("N", i), b, (i - 1) % NI)
                        if pair == N_AT and i == 3 and more:
                            put_v(b.plus(1), "V", b, None)
                        if more:
                            maxima(b.plus(1), b, i, pair, None, pair == 1)
                        if pair == 1 and more:
                            dve.wait_ge(first_reduced, b.at(NI * b.n + i + NI, NI))
                        if pair == 1 and (more or i == 0):
                            max_rows(b if i == 0 else b.plus(1), ("S", i, 1), b, (i - 1) % NI, None)
                        if pair == 2 and i in (1, 2) and most:
                            split_qk(b.plus(2), i - 1)
                        if pair == 3 and i == 3 and b.n > 0:
                            add_out(b.plus(-1), b)
                    period = NI * (b.n - EXPERTS_AT) + i - 1
                    if period >= 0:
                        for n in range(GATHERS * period, GATHERS * (period + 1)):
                            add_expert(n)

            loops(dve, step, experts)
            for n in range(2 * NT - GATHERS, 2 * NT):
                add_expert(n)
            norm(Batch(NB - 1), "N", None, NI - 1, "epi")
            add_out(Batch(NB - 1), None, "epi")


        @block.tensor
        def _(pe):
            def fill(key, b, where=None):
                bank, n = slot(key, b, where)
                wait(pe, wk_free[bank], n - 1)
                return bank

            def scores(b, key_b, i, at, where=None, turns=None, beside=None):
                if beside is not None:
                    n = ring(("T", i, at, 0), beside)
                    if at == 0:
                        pe.wait_ge(mrows[i], beside.at(32 * (beside.n + 1), 32))
                    pe.wait_ge(st_free, n + 2 - ST_BANKS)
                if key_b is not None or where is not None:
                    w = fill(("S", i, at), key_b, where)
                if turns is not None:
                    of, ti = turns
                    pe.wait_ge(nm_done, of.at(2 * (NI * of.n + ti + 1), 2 * NI))
                    last = nc.tensor.matmul(wk[0:G * TJ, w, 0, 3 * P:4 * P], nm[ti % 2][:, :, :].rearrange("p g j -> p (g j)"),
                                            ident[:, :], start=True, stop=True, skip_group_check=True)
                    last.then_inc(maxima_turned, 1)
                    if b.n >= NB:
                        pe.wait_ge(maxima_turned, of.at(NI * of.n + ti + 1, NI))
                        pe.sem_inc(wk_full[w], 1)
                gp, c = pair_at(at)
                by_q = ([(P, 1), (0, 0)] if c == 0 else [(0, c + 1)]) if b.n < NB and (key_b or where) else []
                by_k = CHUNKS[at % 3][::-1] if beside is not None else []
                for piece in range(2):
                    if piece < len(by_k):
                        col, kt, width = by_k[piece]
                        q, k = stack_q[beside.n % 2], stack_k[beside.n % 2]
                        for h in range(2):
                            r = slice(32 * (2 * (at // 3) + h), 32 * (2 * (at // 3) + h) + 32)
                            last = nc.tensor.matmul(st[:, (n + h) % ST_BANKS, col:col + width],
                                                    k[r, i, kt * P:kt * P + P], q[r, i, kt * P:S],
                                                    start=True, stop=True, skip_group_check=True)
                            if piece == len(by_k) - 1:
                                last.then_inc(st_full, 1)
                    if piece < len(by_q):
                        col, j = by_q[piece]
                        q, k = stack_q[b.n % 2], stack_k[b.n % 2]
                        for h in range(2):
                            r, width = slice(32 * (2 * gp + h), 32 * (2 * gp + h) + 32), (j + 1) * P
                            out = wk[:, w, h, col:col + width]
                            nc.tensor.matmul(out, q[r, i, j * P:j * P + P], k[r, i, 0:width],
                                             start=piece == 0, stop=False, skip_group_check=True)
                if by_q:
                    for h in range(2):
                        if c == 0:
                            diag, mask = wk[:, w, h, :].rearrange("p (a t) -> p a t", a=2)[:, :, 0:P], maskb[:, 3:5, :]
                        else:
                            diag, mask = wk[:, w, h, P:(c + 2) * P], maskb[:, 3 - c:4, :]
                        last = nc.tensor.matmul(diag, identb[:, :], mask, start=False, stop=True, skip_group_check=True)
                    last.then_inc(wk_full[w], 1)

            def weigh(b, i, tiles):
                pe.wait_ge(masked, b.at(8 * (NI * b.n + i) + (5 if tiles[-1] == 0 else 6 if tiles[-1] == 1 else 8), 8 * NI))
                if 0 in tiles:
                    if i == 0:
                        pe.wait_ge(v_ready, b.at(b.n + 1, 1))
                    wait(pe, o_evac, b.at(NI * b.n + i, NI))
                for c in range(3):
                    for at, kt, w in CHUNKS[c]:
                        if kt in tiles:
                            for g in range(G):
                                o = CHUNK_AT[c] + at
                                last = nc.tensor.matmul(po[32 * g:32 * g + 32, kt * P:S], v32[b.n % 2][:, kt, 4 * i + g, :],
                                                        probs[i % 2][:, g, o:o + w], start=kt == 0, stop=kt == TJ - 1,
                                                        skip_group_check=True)
                if TJ - 1 in tiles:
                    last.then_inc(pv_done, 1)

            def turn_o(b, key, key_b, i, where=None):
                pe.wait_ge(o_evac, b.at(NI * b.n + i + 1, NI))
                bank = fill(key, key_b, where)
                for j in range(TJ):
                    last = nc.tensor.transpose(wk[:, bank, 0, j * P:j * P + P], o_sb[i % 2][:, j * P:j * P + P], ident[:, :])
                last.then_inc(wk_full[bank], 1)

            def project(b, k, where=None, halves=range(2)):
                pe.wait_ge(xnT_ready, b.n + 1)
                for h in halves:
                    m = 2 * k + h
                    n = ring(("QK"[k], h, b.n), None, where) if where else ring(("QK"[k], h), b.plus(-2))
                    wait(pe, st_free, n + 1 - ST_BANKS)
                    nc.tensor.matmul(st[:, n % ST_BANKS, :], w_sb[:, m * D:m * D + D], xnT[:, S * b.n:S * b.n + S],
                                     start=True, stop=True).then_inc(st_full, 1)

            def project_v(b, key, key_b, where=None):
                pe.wait_ge(xnT_ready, b.n + 1)
                bank = fill(key, key_b, where)
                for j in range(TJ):
                    last = nc.tensor.matmul(wk[:, bank, 0, j * D:j * D + D], xnT[:, S * b.n + j * P:S * b.n + j * P + P],
                                            w_sb[:, 4 * D:5 * D], start=True, stop=True)
                last.then_inc(wk_full[bank], 1)

            def turn_attn(b, key_b, where=None):
                pe.wait_ge(attn_done, b.at(NI * (b.n + 1), NI))
                n = ring("AT", key_b, where)
                pe.wait_ge(st_free, n + 1 - ST_BANKS)
                for j in range(TJ):
                    last = nc.tensor.transpose(st[:, n % ST_BANKS, j * P:j * P + P], attn[b.n % 2][:, j, :], ident[:, :])
                last.then_inc(st_full, 1)

            def project_out(b, key_b, where=None):
                pe.wait_ge(st_free, ring("AT", key_b.plus(0) if key_b else None, where) + 1)
                bank = fill("OP", key_b, where)
                for j in range(TJ):
                    last = nc.tensor.matmul(wk[:, bank, 0, j * D:j * D + D], attnT[:, j * P:j * P + P], wo_sb[:, :],
                                            start=True, stop=True)
                last.then_inc(wk_full[bank], 1)

            def turn_x(b):
                pe.wait_ge(xn_ready, TJ * (b + 1))
                bank = fill(("XT", b), None, "pro")
                for j in range(TJ):
                    last = nc.tensor.transpose(wk[:, bank, 0, j * P:j * P + P], xn[:, TJ * b + j, :], ident[:, :])
                last.then_inc(wk_full[bank], 1)

            pe.wait_ge(ident_ready, 1)
            turn_x(0)
            turn_x(1)
            pe.wait_ge(weights_loaded, 32)
            for b in (Batch(0), Batch(1)):
                for k in range(2):
                    project(b, k, "pro")
                if b.n == 0:
                    project_v(b, ("V", 0), None, "pro")
            def wait_stack(b, i):
                pe.wait_ge(stacked[i], b.at(PIECES * (b.n + 1), PIECES))

            def first_scores(i):
                wait_stack(Batch(0), i)
                for pair in range(PAIRS):
                    scores(Batch(0), None, i, pair, "pro", (Batch(0), i - 1) if pair == 1 and i > 0 else None)

            turn_x(2)
            turn_x(3)
            pe.wait_ge(ones_set, 2)
            pe.wait_ge(pool_consts_set, 5)
            first_scores(0)
            for b in range(4, NB):
                turn_x(b)
            bank = fill("GT", None, "pro")
            pe.wait_ge(consts_loaded, N_CONST)
            pe.wait_ge(xnT_ready, NB)
            for b in range(NB):
                g = b % 4
                last = nc.tensor.matmul(wk[32 * g:32 * g + 32, bank, b // 4, :], gw_sb[:, :], xnT[:, b * S:b * S + S],
                                        start=True, stop=True, skip_group_check=True)
            last.then_inc(wk_full[bank], 1)
            first_scores(1)
            bank = fill("GL", None, "pro")
            pe.wait_ge(gate_scores_ready, 1)
            for half in range(2):
                for j in range(TJ):
                    last = nc.tensor.transpose(wk[:, bank, half, j * P:j * P + P], gt[:, half, j * P:j * P + P], ident[:, :])
            last.then_inc(wk_full[bank], 1)
            first_scores(2)
            bank = fill("CT", None, "pro")
            pe.wait_ge(either_ready, 1)
            flat = either[:, :, :].rearrange("p t e -> p (t e)")
            nc.tensor.matmul(wk[:, bank, 0, 0:NT * E], ones, flat, start=True, stop=True)
            nc.tensor.matmul(wk[:, bank, 0, NT * E:2 * NT * E], above, flat, start=True, stop=True).then_inc(wk_full[bank], 1)
            first_scores(3)

            def step(b):
                more, most = b.n + 1 < NB, b.n + 2 < NB
                b1, b2 = b.plus(1), b.plus(2)
                for i in range(NI):
                    prev, weighs = (b if i else b.plus(-1)), i > 0 or b.n > 0
                    if more:
                        wait_stack(b1, i)
                    for pair in range(PAIRS):
                        if pair == N_AT and weighs:
                            turn_o(prev, ("N", i), b, (i - 1) % NI)
                        if pair == N_AT and i == 3 and more:
                            project_v(b1, "V", b)
                        turned = (b if i == 0 else b1, (i - 1) % NI) if pair == 1 and (more or i == 0) else None
                        scores(b1, b if more or turned else None, i, pair, None, turned, beside=b)
                        if pair < 3 and weighs:
                            weigh(prev, (i - 1) % NI, ((0,), (1,), (2, 3))[pair])
                        if pair in (3, 4) and i < 2 and most:
                            project(b2, i, halves=(pair - 3,))
                        if pair == 3 and i == 3 and b.n > 0:
                            project_out(b.plus(-1), b)
                        if pair == 4 and i == 2 and b.n > 0:
                            turn_attn(b.plus(-1), b)

            def turn_xg(k):
                pe.wait_ge(block_loaded[k.q], k.landed())
                wait(pe, xgT_ready, k.plus(-1))
                nc.tensor.transpose(xT_ps[k.p][:, 0:P], xg[k.q][:, :], ident[:, :]).then_inc(block_turned, 1)

            def up(k):
                pe.wait_ge(w1_copied, k.plus(1))
                pe.wait_ge(xgT_ready, k.plus(1))
                wait(pe, gelu_done, k.plus(-1))
                for c in range(FC):
                    last = nc.tensor.matmul(h_ps[k.p][:, c * P:c * P + P], w1_e[k.p][:, c * P:c * P + P], xgT[k.p][:, :],
                                            start=True, stop=True)
                last.then_inc(up_done, 1)

            def down(k):
                pe.wait_ge(w2_copied, k.plus(1))
                pe.wait_ge(gelu_done, k.plus(1))
                wait(pe, y_ready, k.plus(-1))
                for c in range(FC):
                    last = nc.tensor.matmul(y_ps[k.p][:, 0:D], h[k.p][:, c, :], w2_e[k.p][:, c * D:c * D + D],
                                            start=c == 0, stop=c == FC - 1)
                last.then_inc(down_done, 1)

            def step_x(k, more):
                if more:
                    turn_xg(k.later(2))
                if k.turn is not None or k.n + 1 < BLOCKS:
                    up(k.later(1))
                down(k)

            def experts():
                pe.wait_ge(st_free, RING_START[EXPERTS_AT])
                pe.wait_ge(o_evac, NI * EXPERTS_AT - 1)
                for k in range(SLOTS):
                    pe.wait_ge(wk_free[k], len(range(k, START[EXPERTS_AT], SLOTS)))
                turn_xg(Block(0))
                turn_xg(Block(1))
                up(Block(0))
                blocks(pe, step_x, 2)
                pe.wait_ge(y_ready, BLOCKS)

            loops(pe, step, experts)
            for tiles in ((0,), (1,), (2, 3)):
                weigh(Batch(NB - 1), NI - 1, tiles)
            turn_o(Batch(NB - 1), "N", None, NI - 1, "epi")
            turn_attn(Batch(NB - 1), None, "epi")
            project_out(Batch(NB - 1), None, "epi")


def kernel(**inputs):
    import numpy as _np
    import concourse.bacc as _bacc
    from concourse import mybir as _mybir
    from concourse.bass_utils import run_bass_kernel_spmd as _run

    w = _np.asarray(inputs["L0_attn_qkv_w"])
    bias = _np.asarray(inputs["L0_attn_qkv_b"])
    turned = _np.arange(D).reshape(H, 2, HALF)[:, ::-1].reshape(D)
    wq, wk, wv = w[0:D], w[D:2 * D], w[2 * D:3 * D]
    bq, bk, bv = bias[0:D], bias[D:2 * D], bias[2 * D:3 * D]
    named = {
        "x": inputs["L0_attn_x"],
        "wqkv": _np.concatenate([wq, wq[turned], wk, wk[turned], wv]).T,
        "qkb": _np.stack([bq, bq[turned], bk, bk[turned]], 1),
        "vb": bv,
        "wo": _np.asarray(inputs["L0_attn_out_w"]).T,
        "ob": inputs["L0_attn_out_b"],
        "rope": rope_tables(),
        "gw": _np.concatenate([_np.asarray(inputs["L0_ffn_gate_w"]), _np.zeros((D, 32 - E), _np.float32)], 1),
        "w1": _np.concatenate([_np.asarray(inputs["L0_ffn_w1"]).transpose(1, 0, 2),
                               _np.asarray(inputs["L0_ffn_b1"]).reshape(E, FC, P).transpose(2, 0, 1)], 2),
        "w2": _np.asarray(inputs["L0_ffn_w2"]).reshape(E, FC, P, D).transpose(2, 0, 1, 3),
        "b2": inputs["L0_ffn_b2"],
        "route": routing_tables(),
    }
    nc = _bacc.Bacc("TRN2", target_bir_lowering=False, num_devices=1)
    arrays, args = {}, []
    for name, a in named.items():
        a = _np.ascontiguousarray(a)
        arrays[f"in_{name}_dram"] = a
        args.append(nc.dram_tensor(f"in_{name}_dram", a.shape, _mybir.dt.from_np(a.dtype), kind="ExternalInput").ap())
    args.append(nc.dram_tensor("out_0_dram", (NB, S, D), _mybir.dt.float32, kind="ExternalOutput").ap())
    block_kernel(nc, *args)
    r = _run(nc, [arrays], core_ids=[0])
    return r.results[0]["out_0_dram"]
```
